# Optimizing a Trainium2 kernel written in Bass

```python
import numpy as np
import jax
import jax.numpy as jnp

def _softmax(x, axis=-1):
    return jax.nn.softmax(x, axis=axis)

def _gelu(x):
    return jax.nn.gelu(x, approximate=True)

def _silu(x):
    return jax.nn.silu(x)

def _sigmoid(x):
    return jax.nn.sigmoid(x)

def _layernorm(x, axis=-1, eps=1e-05):
    m = jnp.mean(x, axis=axis, keepdims=True)
    v = jnp.var(x, axis=axis, keepdims=True)
    return (x - m) / jnp.sqrt(v + eps)

def _scatter_add(tgt, idx, src, axis=0):
    return tgt.at[idx].add(src)

def _segment_sum(src, seg, n):
    return jax.ops.segment_sum(src, seg, n)
kernel_name = 'mk_xattn_ffn_d1_seqx_r2_9a55a3'

def setup_inputs(seed: int=0):
    np.random.seed(seed)
    _w = jnp.asarray

    def _rec_inputs():
        import jax
        import jax.numpy as jnp
        _rk = jax.random.key(seed)
        x = -0.0002928 + 1 * jax.random.normal(jax.random.fold_in(_rk, 1), (2, 2048, 512), jnp.float32)
        _lenS = 2048 - jax.random.randint(jax.random.fold_in(_rk, 7), (2,), 0, max(1, 2048 // 4) + 1, jnp.int32)
        _lenS2 = 77 - jax.random.randint(jax.random.fold_in(_rk, 8), (2,), 0, max(1, 77 // 4) + 1, jnp.int32)
        _ctx_1024P = jax.random.normal(jax.random.fold_in(_rk, 11), (2, 16, 512), jnp.float32)
        _ctx_1024c = jax.random.dirichlet(jax.random.fold_in(_rk, 511), 0.3 * jnp.ones((16,), jnp.float32), (2, 77))
        _ctx_1024t = jnp.einsum('bsk,bkd->bsd', _ctx_1024c, _ctx_1024P)
        _ctx_1024t = _ctx_1024t * jax.lax.rsqrt(jnp.mean(jnp.square(_ctx_1024t)) + 1e-12) * 0.953939
        ctx_1024 = -1.39393e-06 + 0.999914 * (_ctx_1024t + 0.3 * jax.random.normal(jax.random.fold_in(_rk, 611), (2, 77, 512), jnp.float32))
        return (x, ctx_1024)
    x, ctx_1024 = _rec_inputs()

    def _L0_xattn_setup():
        import jax, jax.numpy as jnp
        import numpy as np
        D_MODEL = 512
        N_HEADS = 16
        D_KEYS = D_MODEL // N_HEADS
        key = jax.random.key(seed)
        ks = jax.random.split(key, 11)
        B, L, S = (2, 1024, 1024)
        inp = {'queries': jax.random.normal(ks[0], (B, L, D_MODEL), dtype=jnp.float32), 'keys': jax.random.normal(ks[1], (B, S, D_MODEL), dtype=jnp.float32), 'values': jax.random.normal(ks[2], (B, S, D_MODEL), dtype=jnp.float32), 'Wq': jax.random.normal(ks[3], (D_MODEL, D_MODEL), dtype=jnp.float32) / np.sqrt(D_MODEL), 'bq': jax.random.normal(ks[4], (D_MODEL,), dtype=jnp.float32) / np.sqrt(D_MODEL), 'Wk': jax.random.normal(ks[5], (D_MODEL, D_MODEL), dtype=jnp.float32) / np.sqrt(D_MODEL), 'bk': jax.random.normal(ks[6], (D_MODEL,), dtype=jnp.float32) / np.sqrt(D_MODEL), 'Wv': jax.random.normal(ks[7], (D_MODEL, D_MODEL), dtype=jnp.float32) / np.sqrt(D_MODEL), 'bv': jax.random.normal(ks[8], (D_MODEL,), dtype=jnp.float32) / np.sqrt(D_MODEL), 'Wo': jax.random.normal(ks[9], (D_MODEL, D_MODEL), dtype=jnp.float32) / np.sqrt(D_MODEL), 'bo': jax.random.normal(ks[10], (D_MODEL,), dtype=jnp.float32) / np.sqrt(D_MODEL)}
        return inp
    _L0_xattn_all = _L0_xattn_setup()
    _L0_xattn_in = {k: v for k, v in _L0_xattn_all.items() if k in ('Wq', 'bq', 'Wk', 'bk', 'Wv', 'bv', 'Wo', 'bo')}
    del _L0_xattn_all

    def _L0_ffn_setup():
        import jax, jax.numpy as jnp
        import numpy as np
        B, T, D = (2, 1024, 512)
        DCD = 2048
        RET = 128
        NEXP = 2048
        NKEYS = 64
        H = 4
        KPH = 8
        key = jax.random.key(seed)
        ks = jax.random.split(key, 10)
        s = lambda k, shape, scale: jax.random.normal(k, shape, jnp.float32) * scale
        return {'hidden_states': jax.random.normal(ks[0], (B, T, D), jnp.float32), 'Wg': s(ks[1], (D, DCD), 0.02), 'bg': jnp.zeros((DCD,), jnp.float32), 'Wu': s(ks[2], (D, DCD), 0.02), 'bu': jnp.zeros((DCD,), jnp.float32), 'Wd': s(ks[3], (DCD, D), 0.02), 'bd': jnp.zeros((D,), jnp.float32), 'Wq': s(ks[4], (D, RET * H), 0.02), 'keys': s(ks[5], (H, NKEYS, 2, RET // 2), 0.02), 'down_embed': s(ks[6], (NEXP, D), 0.02), 'up_embed': s(ks[7], (NEXP, D), 0.02)}
    _L0_ffn_all = _L0_ffn_setup()
    _L0_ffn_in = {k: v for k, v in _L0_ffn_all.items() if k in ('Wg', 'bg', 'Wu', 'bu', 'Wd', 'bd', 'Wq', 'keys', 'down_embed', 'up_embed')}
    del _L0_ffn_all
    return {'x': x, 'ctx_1024': ctx_1024, 'L0_xattn_Wq': _L0_xattn_in['Wq'], 'L0_xattn_bq': _L0_xattn_in['bq'], 'L0_xattn_Wk': _L0_xattn_in['Wk'], 'L0_xattn_bk': _L0_xattn_in['bk'], 'L0_xattn_Wv': _L0_xattn_in['Wv'], 'L0_xattn_bv': _L0_xattn_in['bv'], 'L0_xattn_Wo': _L0_xattn_in['Wo'], 'L0_xattn_bo': _L0_xattn_in['bo'], 'L0_ffn_Wg': _L0_ffn_in['Wg'], 'L0_ffn_bg': _L0_ffn_in['bg'], 'L0_ffn_Wu': _L0_ffn_in['Wu'], 'L0_ffn_bu': _L0_ffn_in['bu'], 'L0_ffn_Wd': _L0_ffn_in['Wd'], 'L0_ffn_bd': _L0_ffn_in['bd'], 'L0_ffn_Wq': _L0_ffn_in['Wq'], 'L0_ffn_keys': _L0_ffn_in['keys'], 'L0_ffn_down_embed': _L0_ffn_in['down_embed'], 'L0_ffn_up_embed': _L0_ffn_in['up_embed']}

def reference(x, ctx_1024, L0_xattn_Wq, L0_xattn_bq, L0_xattn_Wk, L0_xattn_bk, L0_xattn_Wv, L0_xattn_bv, L0_xattn_Wo, L0_xattn_bo, L0_ffn_Wg, L0_ffn_bg, L0_ffn_Wu, L0_ffn_bu, L0_ffn_Wd, L0_ffn_bd, L0_ffn_Wq, L0_ffn_keys, L0_ffn_down_embed, L0_ffn_up_embed):
    import jax
    import jax.numpy as jnp

    def _L0_xattn_ref(queries, keys, values, Wq, bq, Wk, bk, Wv, bv, Wo, bo):
        import jax, jax.numpy as jnp
        import numpy as np
        D_MODEL = 512
        N_HEADS = 16
        D_KEYS = D_MODEL // N_HEADS
        B, L, _ = queries.shape
        S = keys.shape[1]
        H, E = (N_HEADS, D_KEYS)
        scale = E ** (-0.5)
        q = (queries @ Wq.T + bq).reshape(B, L, H, E)
        k = (keys @ Wk.T + bk).reshape(B, S, H, E)
        v = (values @ Wv.T + bv).reshape(B, S, H, E)
        scores = jnp.einsum('blhe,bshe->bhls', q, k)
        attn = jax.nn.softmax(scores * scale, axis=-1)
        out = jnp.einsum('bhls,bshe->blhe', attn, v).reshape(B, L, H * E)
        return out @ Wo.T + bo

    def _L0_ffn_ref(hidden_states, Wg, bg, Wu, bu, Wd, bd, Wq, keys, down_embed, up_embed):
        import jax, jax.numpy as jnp
        import numpy as np
        B, T, D = (2, 1024, 512)
        DCD = 2048
        RET = 128
        NEXP = 2048
        NKEYS = 64
        H = 4
        KPH = 8
        b, t, d = hidden_states.shape
        q = (hidden_states @ Wq).reshape(b, t, 2, H, RET // 2)
        sim = jnp.einsum('btphn,hkpn->pbthk', q, keys)
        sc, ix = jax.lax.top_k(sim, KPH)
        sx, sy = (sc[0], sc[1])
        ixx, ixy = (ix[0], ix[1])
        all_sc = (sx[..., :, None] + sy[..., None, :]).reshape(b, t, H, KPH * KPH)
        all_ix = (ixx[..., :, None] * NKEYS + ixy[..., None, :]).reshape(b, t, H, KPH * KPH)
        scores, pk = jax.lax.top_k(all_sc, KPH)
        idx = jnp.take_along_axis(all_ix, pk, axis=-1)
        de = down_embed[idx]
        ue = up_embed[idx]
        w = jnp.einsum('btd,bthkd->bthk', hidden_states, de)
        w = jax.nn.silu(w) * jax.nn.softmax(scores, axis=-1)
        experts_states = jnp.einsum('bthk,bthkd->btd', w, ue)
        mlp = jax.nn.silu(hidden_states @ Wg + bg) * (hidden_states @ Wu + bu) @ Wd + bd
        return mlp + experts_states
    x = x + _L0_xattn_ref(_layernorm(x, axis=-1), ctx_1024, ctx_1024, L0_xattn_Wq, L0_xattn_bq, L0_xattn_Wk, L0_xattn_bk, L0_xattn_Wv, L0_xattn_bv, L0_xattn_Wo, L0_xattn_bo)
    x = x + _L0_ffn_ref(_layernorm(x, axis=-1), L0_ffn_Wg, L0_ffn_bg, L0_ffn_Wu, L0_ffn_bu, L0_ffn_Wd, L0_ffn_bd, L0_ffn_Wq, L0_ffn_keys, L0_ffn_down_embed, L0_ffn_up_embed)
    return x

_drawn_inputs = setup_inputs


def setup_inputs(seed=0):
    import zlib

    import numpy as np

    out = dict(_drawn_inputs(seed))
    spreads = {'L0_ffn_bg': (0.0, 0.396), 'L0_ffn_bu': (0.0, 0.405), 'L0_ffn_bd': (0.0, 0.1)}
    factors = {'L0_xattn_bq': 5.765,
     'L0_xattn_bk': 8.0,
     'L0_ffn_Wq': 8.0,
     'L0_ffn_keys': 8.0,
     'L0_ffn_down_embed': 6.266,
     'L0_ffn_up_embed': 6.61}
    for name, (base, spread) in spreads.items():
        noise = np.random.default_rng([zlib.crc32(name.encode()), seed]).standard_normal(out[name].shape)
        drawn = base * np.exp(spread * noise) if base else spread * noise
        out[name] = jnp.asarray(drawn.astype(out[name].dtype))
    for name, factor in factors.items():
        out[name] = (out[name] * factor).astype(out[name].dtype)
    return out
```

```python
from contextlib import ExitStack

import concourse.bass as bass
from concourse import mybir

B, T, D = 2, 2048, 512
S, NH, E = 77, 16, 32
F = 2048
NEXP, H, NK, TOP = 2048, 4, 64, 8
P = 128
EPS = 1e-5
KD = D // P
FB = F // P
EB = NEXP // P
ST = 512
TT = ST // P
NST = B * T // ST
HG = P // E
SW = HG * S
NS = NH * S
NC = -(-NS // P)
VW = 3 * E
NX = NEXP // NK
RING = 5
SLOT = 2048
HALF = SLOT // 2
FAR = -3.0e38


def first_head(c):
    return (P * c) // S


def last_head(c):
    return min(NH - 1, (P * c + P - 1) // S)


class Engine:

    def __init__(self, engine, sem):
        self.engine, self.sem, self.count, self.seen = engine, sem, 0, {}

    def wait(self, *tokens):
        for t in tokens:
            if t is None:
                continue
            sem, value = t
            if self.seen.get(id(sem), 0) < value:
                self.seen[id(sem)] = value
                self.engine.wait_ge(sem, value)

    def do(self, make, *tokens):
        self.wait(*tokens)
        self.count += 1
        make(self.engine).then_inc(self.sem, 1)
        return (self.sem, self.count)

    def quiet(self, make, *tokens):
        self.wait(*tokens)
        make(self.engine)

    def last(self):
        return (self.sem, self.count) if self.count else None


class Dma:

    def __init__(self, sem):
        self.sem, self.count = sem, 0

    def start(self, eng, out, in_, *tokens):
        eng.wait(*tokens)
        self.count += 16
        eng.engine.dma_start(out, in_).then_inc(self.sem, 16)
        return (self.sem, self.count)


def program(nc, x, ctx_in, aWq, abq, aWk, abk, aWv, abv, aWo, abo,
            Wg, bg, Wu, bu, Wd, bd, rWq, rkeys, down, up, out):
    f32, f32r, u32 = mybir.dt.float32, mybir.dt.float32r, mybir.dt.uint32
    ALU, ACT, AX = mybir.AluOpType, mybir.ActivationFunctionType, mybir.AxisListType

    stack = ExitStack()
    with stack:
        def sb(name, shape, dt=f32):
            return stack.enter_context(nc.sbuf_tensor(name, shape, dt))

        def sem(name):
            return stack.enter_context(nc.semaphore(name))

        ring = [sb(f"ring{i}", [P, SLOT], f32r) for i in range(RING)]
        raw = [sb(f"raw{i}", [P, HALF]) for i in range(2)]
        ident = sb("ident", [P, P])
        keysH, keysL = sb("keysH", [P, NS], f32r), sb("keysL", [P, NS], f32r)
        valsH, valsL = sb("valsH", [P, NC * VW], f32r), sb("valsL", [P, NC * VW], f32r)
        xt = sb("xt", [P, TT, D])
        zTH, zTL = sb("zTH", [P, KD, ST], f32r), sb("zTL", [P, KD, ST], f32r)
        sims = sb("sims", [P, TT, 2 * H * NK])
        bias_col = sb("bias_col", [P, 2 * KD + 2 * FB])
        bo_row, bd_row = sb("bo_row", [P, D]), sb("bd_row", [P, D])
        iota = sb("iota", [P, NK])
        rank_code = sb("rank_code", [P, TOP])
        split = sb("split", [P, 2 * KD * ST + 2 * NC * P + 2 * KD * P], f32r)
        plain = sb("plain", [P, TT * NEXP + 2 * NEXP + 4 * ST])
        small = sb("small", [P, 2880])

        qH = split[:, 0:KD * ST].rearrange("p (k t) -> p k t", k=KD)
        qL = split[:, KD * ST:2 * KD * ST].rearrange("p (k t) -> p k t", k=KD)
        a = 2 * KD * ST
        eH = split[:, a:a + NC * P].rearrange("p (c t) -> p c t", c=NC)
        eL = split[:, a + NC * P:a + 2 * NC * P].rearrange("p (c t) -> p c t", c=NC)
        a += 2 * NC * P
        oH = split[:, a:a + KD * P].rearrange("p (k t) -> p k t", k=KD)
        oL = split[:, a + KD * P:a + 2 * KD * P].rearrange("p (k t) -> p k t", k=KD)
        hidH = [split[:, i * ST:(i + 1) * ST] for i in (0, 1)]
        hidL = [split[:, i * ST:(i + 1) * ST] for i in (2, 3)]

        probs = [plain[:, i * NC * P:(i + 1) * NC * P] for i in range(2)]
        att = plain[:, 2 * NC * P:2 * NC * P + D]
        zn = plain[:, 4096:4096 + TT * D].rearrange("p (t d) -> p t d", t=TT)
        dense = plain[:, 0:TT * NEXP].rearrange("p (t e) -> p t e", t=TT)
        a = TT * NEXP
        tmpV = plain[:, a:a + NEXP]
        tmpG = plain[:, a + NEXP:a + 2 * NEXP]
        a += 2 * NEXP
        gate = [plain[:, a + i * ST:a + (i + 1) * ST] for i in (0, 1)]
        hid = [plain[:, a + i * ST:a + (i + 1) * ST] for i in (2, 3)]

        bank = [stack.enter_context(nc.psum_tensor(f"bank{i}", [P, 512], f32)) for i in range(8)]
        bank_free = [[] for _ in range(8)]

        slots_dram = []
        kv_dram = nc.dram_tensor("kv_scratch", (B, P, 2 * NS + 2 * NC * VW), f32).ap()

        PE, DVE = Engine(nc.tensor, sem("s_tensor")), Engine(nc.vector, sem("s_vector"))
        ACTE, POOL = Engine(nc.scalar, sem("s_scalar")), Engine(nc.gpsimd, sem("s_pool"))
        SP = Engine(nc.sync, None)
        d_ring = [Dma(sem(f"s_ring{i}")) for i in range(RING)]
        d_raw = [Dma(sem(f"s_raw{i}")) for i in range(2)]
        d_save = [Dma(sem(f"s_save{i}")) for i in range(RING)]
        d_x, d_const, d_kv, d_prep, d_out = (
            Dma(sem(n)) for n in ("s_x", "s_const", "s_kv", "s_prep", "s_out"))

        def f(ap):
            return ap.bitcast(f32)

        def mm(o, l, r, first, final, *tokens, loose=False):
            PE.quiet(lambda e: e.matmul(o, l, r, start=first, stop=final, skip_group_check=loose), *tokens)

        def mm_end(o, l, r, first, final, *tokens, loose=False):
            return PE.do(lambda e: e.matmul(o, l, r, start=first, stop=final, skip_group_check=loose),
                         *tokens)

        def three(o, lH, lL, rH, rL, first, final, loose=False):
            mm(o, lH, rH, first, False, loose=loose)
            mm(o, lH, rL, False, False, loose=loose)
            return mm_end(o, lL, rH, False, final, loose=loose)

        def take_bank(b):
            PE.wait(*bank_free[b])
            bank_free[b] = []

        def flip(b, col, src, *tokens, rows=P, cols=P):
            return PE.do(lambda e: e.transpose(bank[b][0:cols, col:col + rows], src, ident[0:rows, 0:rows]),
                         *tokens)

        def part(src, high, low, *tokens, col=None):
            if col is None:
                th = ACTE.do(lambda e: e.activation(high, src, ACT.Copy), *tokens)
                tl = DVE.do(lambda e: e.tensor_tensor(low, src, f(high), ALU.subtract), th)
            else:
                th = ACTE.do(lambda e: e.activation(high, src, ACT.Identity, bias=col), *tokens)
                tl = DVE.do(lambda e: e.scalar_tensor_tensor(low, src, col, f(high), ALU.add, ALU.subtract), th)
            return th, tl

        t_id0 = POOL.do(lambda e: e.memset(ident[:, :], 0.0))
        t_id = POOL.do(lambda e: e.affine_select(out=ident[:, :], in_=ident[:, :], compare_op=ALU.not_equal,
                                                 fill=1.0, base=0, pattern=[[-1, P]], channel_multiplier=1), t_id0)
        t_iota = POOL.do(lambda e: e.iota(iota[:, :], pattern=[[1, NK]], base=0, channel_multiplier=0,
                                          allow_small_or_imprecise_dtypes=True))
        t_code = POOL.do(lambda e: e.iota(rank_code[:, :], pattern=[[1, TOP]], base=-TOP, channel_multiplier=0,
                                          allow_small_or_imprecise_dtypes=True))
        nb = 2 * KD + 2 * FB
        braw = small[0:nb, 0:P]
        at = 0
        for src, n in ((abq, KD), (abk, KD), (bg, FB), (bu, FB)):
            t_b = d_const.start(SP, small[at:at + n, 0:P], src.rearrange("(n p) -> n p", p=P))
            at += n
        t_b = d_const.start(SP, bo_row[:, :], abo.unsqueeze(0).to_broadcast([P, D]))
        t_b = d_const.start(SP, bd_row[:, :], bd.unsqueeze(0).to_broadcast([P, D]))
        bv_at = 3 * KD * D + KD * S + D
        bv_row = plain[:, bv_at:bv_at + D]
        t_b = t_bv = d_const.start(SP, bv_row, abv.unsqueeze(0).to_broadcast([P, D]))
        t_f = flip(7, 0, braw, t_b, t_id, rows=nb, cols=P)
        t_bias = DVE.do(lambda e: e.tensor_copy(bias_col[:, :], bank[7][:, 0:nb]), t_f)
        bank_free[7] = [t_bias]
        bq_c = [bias_col[:, k:k + 1] for k in range(KD)]
        bk_c = [bias_col[:, KD + k:KD + k + 1] for k in range(KD)]
        bg_c = [bias_col[:, 2 * KD + k:2 * KD + k + 1] for k in range(FB)]
        bu_c = [bias_col[:, 2 * KD + FB + k:2 * KD + FB + k + 1] for k in range(FB)]

        wkvT = plain[:, 0:2 * KD * D].rearrange("p (w k n) -> p w k n", w=2, k=KD)
        a = 2 * KD * D
        wraw = plain[:, a:a + KD * D].rearrange("p (k n) -> p k n", k=KD)
        a += KD * D
        cT = plain[:, a:a + KD * S].rearrange("p (k n) -> p k n", k=KD)
        a += KD * S
        craw = plain[0:S, a:a + D]
        a += D
        assert a == bv_at
        a += D
        vrow = plain[0:S, a:a + D]
        a += D
        kbd = plain[:, a:a + NS]
        a += NS
        vexp = plain[:, a:a + NC * VW]
        assert a + NC * VW <= TT * NEXP + 2 * NEXP + 4 * ST

        t_wT = None
        for w, W in enumerate((aWk, aWv)):
            t_w = d_prep.start(SP, wraw, W.rearrange("(k p) n -> p k n", p=P), PE.last())
            for k in range(KD):
                b = k % 4
                take_bank(b)
                for r in range(KD):
                    t_f = flip(b, r * P, wraw[:, r, k * P:(k + 1) * P], t_w, t_id)
                t_wT = DVE.do(lambda e, b=b, w=w, k=k: e.tensor_copy(wkvT[:, w, k, :], bank[b][:, :]), t_f)
                bank_free[b] = [t_wT]
        t_saved = None
        for b_ in range(B):
            t_c = d_prep.start(SP, craw, ctx_in[b_], PE.last())
            take_bank(4)
            for k in range(KD):
                t_f = flip(4, k * S, craw[:, k * P:(k + 1) * P], t_c, rows=S, cols=P)
            t_cT = DVE.do(lambda e: e.tensor_copy(cT, bank[4][:, 0:KD * S].rearrange("p (k n) -> p k n", k=KD)), t_f)
            bank_free[4] = [t_cT]
            take_bank(5)
            for k in range(KD):
                t_v = mm_end(bank[5][0:S, :], cT[:, k, :], wkvT[:, 1, k, :], k == 0, k == KD - 1, t_cT, t_wT)
            t_v = DVE.do(lambda e: e.tensor_tensor(vrow, bank[5][0:S, :], bv_row[0:S, :], ALU.add),
                         t_v, t_bv, (d_prep.sem, d_prep.count))
            bank_free[5] = [t_v]
            t_z = DVE.do(lambda e: e.memset(vexp, 0.0), t_saved)
            for h in range(NH):
                r = h * S
                while r < (h + 1) * S:
                    c = r // P
                    n = min((h + 1) * S, (c + 1) * P) - r
                    col = c * VW + (h - first_head(c)) * E
                    t_p = d_prep.start(SP, vexp[r - c * P:r - c * P + n, col:col + E],
                                       vrow[r - h * S:r - h * S + n, h * E:(h + 1) * E], t_v, t_z)
                    r += n
            t_k0 = DVE.do(lambda e: e.memset(kbd, 0.0), t_saved)
            for g in range(KD):
                take_bank(6)
                for k in range(KD):
                    t_k = mm_end(bank[6][:, 0:S], wkvT[:, 0, k, g * P:(g + 1) * P], cT[:, k, :], k == 0, k == KD - 1)
                for r in range(HG):
                    rows = slice(r * E, (r + 1) * E)
                    col = g * SW + r * S
                    t_kb = DVE.do(lambda e, rows=rows, col=col, g=g: e.tensor_scalar(
                        kbd[rows, col:col + S], bank[6][rows, 0:S], bk_c[g][rows, :], None, ALU.add), t_k, t_k0, t_bias)
                bank_free[6] = [t_kb]
            part(kbd, keysH[:, :], keysL[:, :], t_kb, t_saved)
            t_h, t_l = part(vexp, valsH[:, :], valsL[:, :], t_p)
            o = 0
            for src, n in ((keysH, NS), (keysL, NS), (valsH, NC * VW), (valsL, NC * VW)):
                t_saved = d_kv.start(SP, kv_dram[b_, :, o:o + n], f(src[:, :]), t_h, t_l)
                o += n

        uses = ([("wq", i) for i in range(2)] + [("wo", i) for i in range(2)] + [("w2", i) for i in range(2)])
        for i in range(FB):
            uses.append(("gu", i))
            if i % 2 == 0:
                uses.append(("wd", i // 2))
        uses += [("ex", i) for i in range(EB)]
        NU = len(uses)
        slots_dram = nc.dram_tensor("slot_scratch", (NU, P, SLOT), f32).ap()
        slot_ready, slot_free = {}, [None] * RING
        t_written = [None] * NU
        raw_n = [0]
        raw_free = [[], []]
        raw_tok = {}

        def load_raw(*pieces):
            i = raw_n[0] % 2
            raw_n[0] += 1
            SP.wait(*raw_free[i])
            for dst, src in pieces:
                t = d_raw[i].start(SP, dst(raw[i]), src)
            return i, t

        pre = {}

        def prefetch_raw(u):
            kind, i = uses[u]
            if kind == "gu":
                ps = [(lambda r, o=o: r[:, o:o + D].rearrange("p (k n) -> p k n", k=KD),
                       W[:, i * P:(i + 1) * P].rearrange("(k p) n -> p k n", p=P)) for o, W in ((0, Wg), (D, Wu))]
            elif kind == "wd":
                ps = [(lambda r: r[:, :].rearrange("p (k n) -> p k n", k=2),
                       Wd[2 * i * P:(2 * i + 2) * P, :].rearrange("(k p) n -> p k n", p=P))]
            elif kind == "ex":
                ps = [(lambda r, o=o: r[:, o:o + D], W[i * P:(i + 1) * P, :]) for o, W in ((0, down), (D, up))]
            pre[u] = load_raw(*ps)

        def make_slot(u):
            kind, i = uses[u]
            s = u % RING
            hi, lo = ring[s][:, 0:HALF], ring[s][:, HALF:SLOT]
            if kind in ("gu", "wd"):
                j, t = pre.pop(u)
                th, tl = part(raw[j][:, :], hi, lo, t, slot_free[s], t_written[u])
                raw_free[j] = [th, tl]
            elif kind == "ex":
                j, t = pre.pop(u)
                b = 4 + i % 4
                take_bank(b)
                for k in range(KD):
                    t_f = flip(b, k * P, raw[j][:, k * P:(k + 1) * P], t)
                th, tl = part(bank[b][:, :], hi[:, 0:D], lo[:, 0:D], t_f, slot_free[s])
                bank_free[b] = [th, tl]
                th, tl = part(raw[j][:, D:2 * D], hi[:, D:2 * D], lo[:, D:2 * D], t)
                raw_free[j] = [th, tl]
            else:
                W = {"wq": aWq, "wo": aWo, "w2": rWq}[kind]
                if i == 0:
                    for r in range(2):
                        j, t = load_raw((lambda z: z[:, :].rearrange("p (k n) -> p k n", k=2),
                                         W[2 * r * P:(2 * r + 2) * P, :].rearrange("(k p) n -> p k n", p=P)))
                        raw_tok[r] = (j, t)
                for k2 in range(2):
                    k = 2 * i + k2
                    b = 4 + k % 2
                    take_bank(b)
                    if kind != "w2":
                        for r in range(KD):
                            j, t = raw_tok[r // 2]
                            t_f = flip(b, r * P, raw[j][:, (r % 2) * D + k * P:(r % 2) * D + (k + 1) * P], t)
                    else:
                        j, t = raw_tok[k // 2]
                        take_bank(6)
                        for q in range(KD):
                            o = (k % 2) * D + q * P
                            t_f = flip(6, q * P, raw[j][:, o:o + P], t)
                        t_r = DVE.do(lambda e: e.tensor_copy(rqT, bank[6][:, :]), t_f, PE.last())
                        bank_free[6] = [t_r]
                        for q in range(KD):
                            t_f = mm_end(bank[b][:, q * P:(q + 1) * P], rqT[:, q * P:(q + 1) * P],
                                         keyT[:, q * P:(q + 1) * P], True, True, t_r, t_keyT)
                    c = slice(k2 * D, (k2 + 1) * D)
                    th, tl = part(bank[b][:, :], hi[:, c], lo[:, c], t_f, slot_free[s])
                    bank_free[b] = [th, tl]
                if i == 1:
                    raw_free[0] = [PE.last()]
                    raw_free[1] = [PE.last()]
            slot_ready[u] = [th, tl]
            t = d_save[s].start(SP, slots_dram[u], f(ring[s][:, :]), th, tl)
            t_written[u] = t
            saved_slot[s] = t

        saved_slot = [None] * RING
        kblk = small[:, 0:KD * P]
        keyT = plain[:, TT * NEXP:TT * NEXP + KD * P]
        rqT = plain[:, TT * NEXP + KD * P:TT * NEXP + 2 * KD * P]
        t_kz = DVE.do(lambda e: e.memset(kblk, 0.0), PE.last())
        for q in range(KD):
            for r in range(2):
                p_, h = (2 * q + r) // H, (2 * q + r) % H
                t_kp = d_prep.start(SP, kblk[r * NK:(r + 1) * NK, q * P + r * NK:q * P + (r + 1) * NK],
                                    rkeys[h, :, p_, :], t_kz)
        take_bank(7)
        for q in range(KD):
            t_f = flip(7, q * P, kblk[:, q * P:(q + 1) * P], t_kp)
        t_keyT = DVE.do(lambda e: e.tensor_copy(keyT, bank[7][:, :]), t_f, ACTE.last(), t_p)
        bank_free[7] = [t_keyT]

        def fetch(n):
            if n >= NU * NST:
                return
            s = n % RING
            if n < NU:
                make_slot(n)
                for m in (n + 1, n + 2):
                    if m < NU and m not in pre and m > made[0] and uses[m][0] in ("gu", "wd", "ex"):
                        prefetch_raw(m)
                        made[0] = m
            else:
                slot_ready[n] = [d_ring[s].start(SP, f(ring[s][:, :]), slots_dram[n % NU],
                                                 slot_free[s], t_written[n % NU])]

        made = [5]
        used, closed, sent = [0], set(), [RING]

        def open_slot(kind, i):
            n = used[0]
            assert uses[n % NU] == (kind, i), (uses[n % NU], kind, i)
            used[0] += 1
            PE.wait(*slot_ready[n])
            return n, ring[n % RING]

        def close_slot(n, token):
            closed.add(n)
            slot_free[n % RING] = token
            while sent[0] - RING in closed:
                m = sent[0] - RING
                if m < NU:
                    for e in (SP, ACTE, DVE):
                        e.wait(saved_slot[m % RING])
                fetch(sent[0])
                sent[0] += 1

        x_v = x.rearrange("b (s t p) d -> (b s) p t d", t=TT, p=P)
        out_v = out.rearrange("b (s t p) d -> (b s) p t d", t=TT, p=P)
        stats = small[:, 0:TT * 6].rearrange("p (t n) -> p t n", t=TT)
        mv = small[:, 32:32 + TT * 2].rearrange("p (t n) -> p t n", t=TT)
        std = small[:, 48:48 + TT]
        rstd = small[:, 56:56 + TT]
        mx = [small[:, 64 + 64 * i:64 + 64 * i + NH] for i in range(2)]
        den = [small[:, 64 + 64 * i + 16:64 + 64 * i + 32] for i in range(2)]
        rden = [small[:, 64 + 64 * i + 32:64 + 64 * i + 48] for i in range(2)]

        def layernorm(*tokens):
            for t in range(TT):
                ts = DVE.do(lambda e, t=t: e.bn_stats(stats[:, t, :], xt[:, t, :]), *tokens)
                tm = DVE.do(lambda e, t=t: e.bn_aggr(mv[:, t, :], stats[:, t, :]), ts)
            te = DVE.do(lambda e: e.tensor_scalar(std, mv[:, :, 1], EPS, None, ALU.add), tm)
            tq = ACTE.do(lambda e: e.activation(std, std, ACT.Sqrt), te)
            tr = DVE.do(lambda e: e.reciprocal(rstd, std), tq)
            done = []
            for t in range(TT):
                done.append(DVE.do(lambda e, t=t: e.tensor_scalar(
                    zn[:, t, :], xt[:, t, :], mv[:, t, 0:1], rstd[:, t:t + 1], ALU.subtract, ALU.mult), tr))
            return done

        def turn_z(done):
            for k in range(KD):
                b = k
                take_bank(b)
                for t in range(TT):
                    t_f = flip(b, t * P, zn[:, t, k * P:(k + 1) * P], done[t])
                th, tl = part(bank[b][:, :], zTH[:, k, :], zTL[:, k, :], t_f)
                bank_free[b] = [th, tl]
            PE.wait(th, tl)

        t_out = None

        def attention(i):
            everyone = [PE.last(), DVE.last(), ACTE.last(), POOL.last()]
            for e in (PE, DVE, ACTE, POOL):
                e.wait(*everyone)
            t_x = d_x.start(SP, xt[:, :, :], x_v[i], *everyone, t_out)
            t_kv = None
            if i % (NST // B) == 0:
                b_ = i // (NST // B)
                o = 0
                for dst, n in ((keysH, NS), (keysL, NS), (valsH, NC * VW), (valsL, NC * VW)):
                    t_kv = d_kv.start(SP, f(dst[:, :]), kv_dram[b_, :, o:o + n], t_saved, *everyone)
                    o += n
            done = layernorm(t_x)
            t_bo = [POOL.do(lambda e, t=t: e.tensor_tensor(xt[:, t, :], xt[:, t, :], bo_row[:, :], ALU.add), done[t])
                    for t in range(TT)]
            turn_z(done)

            slots = [open_slot("wq", j) for j in range(2)]
            q_bank = []
            for g in range(KD):
                b = 4 + g
                take_bank(b)
                for k in range(KD):
                    w = slots[k // 2][1]
                    o = (k % 2) * D + g * P
                    t_q = three(bank[b][:, :], w[:, o:o + P], w[:, HALF + o:HALF + o + P],
                                zTH[:, k, :], zTL[:, k, :], k == 0, k == KD - 1)
                th, tl = part(bank[b][:, :], qH[:, g, :], qL[:, g, :], t_q, col=bq_c[g])
                bank_free[b] = [th, tl]
            t_qs = [th, tl]
            for n, _ in slots:
                close_slot(n, t_q)
            slots = [open_slot("wo", j) for j in range(2)]

            t_pad = [DVE.do(lambda e, j=j: e.memset(probs[j][:, NS:NC * P], 0.0)) for j in range(2)]
            probs_free = [[], []]

            def scores(t):
                j = t % 2
                tok = slice(t * P, (t + 1) * P)
                for g in range(KD):
                    take_bank(g)
                    PE.wait(*t_qs, t_kv)
                    c = slice(g * SW, (g + 1) * SW)
                    t_s = three(bank[g][:, 0:SW], qH[:, g, tok], qL[:, g, tok], keysH[:, c], keysL[:, c], True, True)
                    v = bank[g][:, 0:SW].rearrange("p (h s) -> p h s", h=HG)
                    hs = slice(g * HG, (g + 1) * HG)
                    pv = probs[j][:, c].rearrange("p (h s) -> p h s", h=HG)
                    t_m = DVE.do(lambda e, v=v, hs=hs: e.tensor_reduce(mx[j][:, hs], v, AX.X, ALU.max), t_s)
                    t_d = DVE.do(lambda e, v=v, hs=hs, pv=pv: e.tensor_tensor(
                        pv, v, mx[j][:, hs].unsqueeze(2).to_broadcast([P, HG, S]), ALU.subtract), t_m, *probs_free[j])
                    bank_free[g] = [t_d]
                t_e = ACTE.do(lambda e: e.activation(probs[j][:, 0:NS], probs[j][:, 0:NS], ACT.Exp, scale=E ** -0.5), t_d)
                t_n = DVE.do(lambda e: e.tensor_reduce(den[j], probs[j][:, 0:NS].rearrange("p (h s) -> p h s", h=NH),
                                                       AX.X, ALU.add), t_e)
                t_r = DVE.do(lambda e: e.reciprocal(rden[j], den[j]), t_n)
                return t_e, t_r

            def values(t, t_e, t_r):
                j = t % 2
                for c0 in range(0, NC, 4):
                    b = 4 + (c0 // 4) % 2
                    n = min(4, NC - c0)
                    take_bank(b)
                    for c in range(c0, c0 + n):
                        t_f = flip(b, (c - c0) * P, probs[j][:, c * P:(c + 1) * P], t_e, *t_pad)
                    ap = lambda z: z[:, c0:c0 + n, :].rearrange("p c t -> p (c t)")
                    th, tl = part(bank[b][:, 0:n * P], ap(eH), ap(eL), t_f)
                    bank_free[b] = [th, tl]
                probs_free[j] = [t_f]
                take_bank(6)
                PE.wait(th, tl)
                for c in range(NC):
                    h0, h1 = first_head(c), last_head(c)
                    w = (h1 - h0 + 1) * E
                    t_o = three(bank[6][:, h0 * E:h0 * E + w], eH[:, c, :], eL[:, c, :],
                                valsH[:, c * VW:c * VW + w], valsL[:, c * VW:c * VW + w],
                                c == 0, c == NC - 1, loose=True)
                t_a = DVE.do(lambda e: e.tensor_tensor(
                    att.rearrange("p (h e) -> p h e", h=NH), bank[6][:, :].rearrange("p (h e) -> p h e", h=NH),
                    rden[j].unsqueeze(2).to_broadcast([P, NH, E]), ALU.mult), t_o, t_r)
                bank_free[6] = [t_a]
                take_bank(7)
                for k in range(KD):
                    t_f = flip(7, k * P, att[:, k * P:(k + 1) * P], t_a)
                th, tl = part(bank[7][:, :], oH.rearrange("p k t -> p (k t)"), oL.rearrange("p k t -> p (k t)"), t_f)
                bank_free[7] = [th, tl]
                take_bank(6)
                PE.wait(th, tl)
                for k in range(KD):
                    w = slots[k // 2][1]
                    o = (k % 2) * D
                    t_w = three(bank[6][:, :], oH[:, k, :], oL[:, k, :], w[:, o:o + D], w[:, HALF + o:HALF + o + D],
                                k == 0, k == KD - 1)
                t_x1 = DVE.do(lambda e: e.tensor_tensor(xt[:, t, :], bank[6][:, :], xt[:, t, :], ALU.add), t_w, t_bo[t])
                bank_free[6] = [t_x1]
                return t_w, t_x1

            pending = scores(0)
            for t in range(TT):
                following = scores(t + 1) if t + 1 < TT else None
                t_w, t_x1 = values(t, *pending)
                pending = following
            for n, _ in slots:
                close_slot(n, t_w)

            done = layernorm(t_x1)
            turn_z(done)
            t_bd = [POOL.do(lambda e, t=t: e.tensor_tensor(xt[:, t, :], xt[:, t, :], bd_row[:, :], ALU.add), done[t])
                    for t in range(TT)]
            slots = [open_slot("w2", j) for j in range(2)]
            t_sim = []
            for t in range(TT):
                b = 4 + t
                take_bank(b)
                for k in range(KD):
                    w = slots[k // 2][1]
                    o = (k % 2) * D
                    tok = slice(t * P, (t + 1) * P)
                    t_s = three(bank[b][:, :], zTH[:, k, tok], zTL[:, k, tok], w[:, o:o + D], w[:, HALF + o:HALF + o + D],
                                k == 0, k == KD - 1)
                t_c = ACTE.do(lambda e, t=t, b=b: e.activation(sims[:, t, :], bank[b][:, :], ACT.Copy), t_s)
                bank_free[b] = [t_c]
                t_sim.append(t_c)
            for n, _ in slots:
                close_slot(n, t_s)
            return t_sim, t_bd

        a = 0
        def room(n):
            nonlocal a
            v = small[:, a:a + n]
            a += n
            return v
        HT, HC = H * TOP, H * TOP * TOP
        top = room(2 * HT)
        index = sb("index", [P, 2 * HT], u32)
        index_f = room(2 * HT)
        cand = room(HC)
        left = room(HC)
        best = room(HT)
        weight = room(HC)
        count = room(HT)
        row = room(HT)
        total, inv = room(H), room(H)
        beyond = room(HT)
        clamp = room(1)
        row_ns = [room(H * NX) for _ in range(2)]
        codes = [room(H * NK) for _ in range(2)]
        exs = [room(2 * H * NK) for _ in range(2)]
        assert a <= 2880

        kept = [sb(f"kept{i}", [P, NEXP], mybir.dt.bfloat16) for i in range(2)]
        kept_free = [None, None]

        def retrieval(t, t_sim, t_dense):
            sim = sims[:, t, :].rearrange("p (g n) -> p g n", g=2 * H)
            top3 = top.rearrange("p (g n) -> p g n", g=2 * H)
            V = DVE.do
            row_n, code, ex = row_ns[t % 2], codes[t % 2], exs[t % 2]
            everyone = t_dense.get(t - 2)
            for g in range(2 * H):
                t1 = V(lambda e, g=g: e.max(top3[:, g, :], sim[:, g, :]), t_sim, everyone)
                t1 = V(lambda e, g=g: e.max_index(index[:, g * TOP:(g + 1) * TOP], top3[:, g, :], sim[:, g, :]), t1)
            t1 = V(lambda e: e.tensor_copy(index_f, index[:, :]), t1)
            yield
            c4 = cand.rearrange("p (h a b) -> p h a b", h=H, a=TOP)
            for h in range(H):
                t2 = V(lambda e, h=h: e.tensor_tensor(
                    c4[:, h, :, :], top3[:, h, :].unsqueeze(2).to_broadcast([P, TOP, TOP]),
                    top3[:, H + h, :].unsqueeze(1).to_broadcast([P, TOP, TOP]), ALU.add), t1)
            c2 = cand.rearrange("p (h n) -> p h n", h=H)
            l2 = left.rearrange("p (h n) -> p h n", h=H)
            b2 = best.rearrange("p (h n) -> p h n", h=H)
            for h in range(H):
                t3 = V(lambda e, h=h: e.max(b2[:, h, :], c2[:, h, :]), t2)
                t3 = V(lambda e, h=h: e.match_replace(l2[:, h, :], b2[:, h, :], c2[:, h, :], FAR), t3)
            yield
            t3 = V(lambda e: e.tensor_tensor(left, left, cand, ALU.is_lt), t3)
            t_n = V(lambda e: e.tensor_reduce(count, left.rearrange("p (r n) -> p r n", n=TOP), AX.X, ALU.add), t3)
            t4 = V(lambda e: e.tensor_tensor(weight.rearrange("p (h n) -> p h n", h=H), c2,
                                             b2[:, :, 0:1].to_broadcast([P, H, TOP * TOP]), ALU.subtract), t3)
            t4 = ACTE.do(lambda e: e.activation(weight, weight, ACT.Exp), t4)
            ex3 = ex.rearrange("p (g n) -> p g n", g=2 * H)
            t5 = V(lambda e: e.tensor_tensor(ex3, sim, top3[:, :, 0:1].to_broadcast([P, 2 * H, NK]), ALU.subtract), t1)
            t5 = ACTE.do(lambda e: e.activation(ex, ex, ACT.Exp), t5)
            yield
            t4 = V(lambda e: e.tensor_tensor(weight, weight, left, ALU.mult), t4)
            t4 = V(lambda e: e.tensor_reduce(row, weight.rearrange("p (r n) -> p r n", n=TOP), AX.X, ALU.add), t4)
            t6 = V(lambda e: e.tensor_reduce(total, row.rearrange("p (h n) -> p h n", h=H), AX.X, ALU.add), t4)
            t6 = V(lambda e: e.reciprocal(inv, total), t6)
            t7 = V(lambda e: e.scalar_tensor_tensor(beyond, index_f[:, 0:HT], float(NX), row, ALU.is_ge, ALU.mult), t6)
            t7 = V(lambda e: e.tensor_tensor(beyond.rearrange("p (h n) -> p h n", h=H), beyond.rearrange("p (h n) -> p h n", h=H),
                                             inv.unsqueeze(2).to_broadcast([P, H, TOP]), ALU.mult), t7)
            t7 = V(lambda e: e.tensor_reduce(clamp, beyond, AX.X, ALU.add), t7)
            t8 = V(lambda e: e.tensor_tensor(ex3[:, 0:H, 0:NX], ex3[:, 0:H, 0:NX],
                                             inv.unsqueeze(2).to_broadcast([P, H, NX]), ALU.mult), t5, t6)
            yield
            one = tmpV[:, 0:H * NX * TOP].rearrange("p (h i r) -> p h i r", h=H, i=NX)
            for h in range(H):
                t9 = V(lambda e, h=h: e.tensor_tensor(
                    one[:, h], iota[:, 0:NX].unsqueeze(2).to_broadcast([P, NX, TOP]),
                    index_f[:, h * TOP:(h + 1) * TOP].unsqueeze(1).to_broadcast([P, NX, TOP]), ALU.is_equal), t8)
                t9 = V(lambda e, h=h: e.tensor_tensor(
                    one[:, h], one[:, h], count[:, h * TOP:(h + 1) * TOP].unsqueeze(1).to_broadcast([P, NX, TOP]), ALU.mult), t9, t_n)
            t9 = V(lambda e: e.tensor_reduce(row_n, tmpV[:, 0:H * NX * TOP].rearrange("p (r n) -> p r n", n=TOP), AX.X, ALU.add), t9)
            yield
            one = tmpV.rearrange("p (h i r) -> p h i r", h=H, i=NK)
            for h in range(H):
                tc = V(lambda e, h=h: e.tensor_tensor(
                    one[:, h], iota[:, :].unsqueeze(2).to_broadcast([P, NK, TOP]),
                    index_f[:, HT + h * TOP:HT + (h + 1) * TOP].unsqueeze(1).to_broadcast([P, NK, TOP]), ALU.is_equal), t9)
                tc = V(lambda e, h=h: e.tensor_tensor(
                    one[:, h], one[:, h], rank_code[:, :].unsqueeze(1).to_broadcast([P, NK, TOP]), ALU.mult), tc)
                if h % 2:
                    yield
            tc = V(lambda e: e.tensor_reduce(code, tmpV.rearrange("p (r n) -> p r n", n=TOP), AX.X, ALU.add), tc)
            tc = V(lambda e: e.tensor_scalar(code, code, float(TOP), None, ALU.add), tc)
            yield
            ready = tc

            i2 = lambda v: v.unsqueeze(2).to_broadcast([P, NX, NK])
            j2 = lambda v: v.unsqueeze(1).to_broadcast([P, NX, NK])
            d3 = dense[:, t, :].rearrange("p (i j) -> p i j", i=NX)
            k = kp = None
            for h in range(H):
                eng, room_ = (DVE, tmpV) if h < 2 else (POOL, tmpG)
                r3 = room_.rearrange("p (i j) -> p i j", i=NX)
                m3 = (room_ if h < 2 else kept[h - 2][:, :]).rearrange("p (i j) -> p i j", i=NX)
                k = V(lambda e: e.tensor_tensor(m3, j2(code[:, h * NK:(h + 1) * NK]),
                                                i2(row_n[:, h * NX:(h + 1) * NX]), ALU.is_lt),
                      ready, k, None if h < 2 else kept_free[h - 2])
                if h >= 2:
                    t_mask, kp = k, POOL.last()
                k = eng.do(lambda e: e.tensor_tensor(r3, m3, i2(ex3[:, h, 0:NX]), ALU.mult), k, kp)
                if h >= 2:
                    kept_free[h - 2] = k
                if h == 0:
                    k = V(lambda e: e.tensor_tensor(d3, r3, j2(ex3[:, H + h, :]), ALU.mult), k)
                else:
                    k = eng.do(lambda e: e.tensor_tensor(r3, r3, j2(ex3[:, H + h, :]), ALU.mult), k)
                    k = eng.do(lambda e: e.tensor_tensor(d3, d3, r3, ALU.add), k)
                if h == 1:
                    k = V(lambda e: e.tensor_tensor(dense[:, t, NEXP - 1:NEXP], dense[:, t, NEXP - 1:NEXP], clamp, ALU.add), k)
                if h >= 2:
                    kp, k = k, t_mask
                yield
            k = kp
            t_dense[t] = k

        def hidden_layers(i, t_sim, t_bd):
            nonlocal t_out
            for e in (DVE, ACTE, POOL):
                e.wait(PE.last(), ACTE.last(), DVE.last())
            for b in range(TT):
                take_bank(b)
            later = []
            t_dense = {}
            n_blocks = FB + EB
            work = (None for t in range(TT) for _ in retrieval(t, t_sim[t], t_dense))
            total_steps, steps = TT * 12, [0]
            hid_free = [None, None]

            def project(n, m, wH, wL, ready, closing):
                PE.wait(*ready)
                for t in range(TT):
                    tok = slice(t * P, (t + 1) * P)
                    k = three(bank[t][:, :], hidH[m][:, tok], hidL[m][:, tok], wH, wL, n == 0, n == n_blocks - 1)
                hid_free[m] = k
                for c in closing:
                    close_slot(c, k)

            wd = None
            for n in range(n_blocks):
                m = n % 2
                b0, b1 = (4, 5) if m == 0 else (6, 7)
                take_bank(b0)
                take_bank(b1)
                if n < FB:
                    su, w = open_slot("gu", n)
                    if n % 2 == 0:
                        wd = open_slot("wd", n // 2)
                    for bb, o in ((b0, 0), (b1, D)):
                        for k in range(KD):
                            c = o + k * P
                            t_g = three(bank[bb][:, :], w[:, c:c + P], w[:, HALF + c:HALF + c + P],
                                        zTH[:, k, :], zTL[:, k, :], k == 0, k == KD - 1)
                        if bb == b0:
                            t_g0 = t_g
                    t_s = ACTE.do(lambda e: e.activation(gate[m], bank[b0][:, :], ACT.Silu, bias=bg_c[n]), t_g0)
                    t_h = DVE.do(lambda e: e.scalar_tensor_tensor(hid[m], bank[b1][:, :], bu_c[n], gate[m], ALU.add, ALU.mult),
                                 t_g, t_s)
                    o = (n % 2) * D
                    w2 = wd[1]
                    second = (w2[:, o:o + D], w2[:, HALF + o:HALF + o + D])
                    closing = [] if n % 2 == 0 else [wd[0]]
                    t_up = t_g
                else:
                    eb = n - FB
                    su, w = open_slot("ex", eb)
                    for k in range(KD):
                        c = k * P
                        t_g = three(bank[b0][:, :], w[:, c:c + P], w[:, HALF + c:HALF + c + P],
                                    zTH[:, k, :], zTL[:, k, :], k == 0, k == KD - 1)
                    for t in range(TT):
                        t_f = flip(b1, t * P, dense[:, t, eb * P:(eb + 1) * P], t_dense[t])
                    t_s = ACTE.do(lambda e: e.activation(gate[m], bank[b0][:, :], ACT.Silu), t_g)
                    t_h = DVE.do(lambda e: e.tensor_tensor(hid[m], bank[b1][:, :], gate[m], ALU.mult), t_f, t_s)
                    second = (w[:, D:2 * D], w[:, HALF + D:HALF + 2 * D])
                    closing = [su]
                bank_free[b0], bank_free[b1] = [t_s], [t_h]
                th, tl = part(hid[m], hidH[m], hidL[m], t_h, hid_free[m])
                if later:
                    project(*later.pop())
                later.append((n, m, *second, (th, tl), closing))
                if n < FB:
                    close_slot(su, t_up)
                while n < FB and len(t_dense) < TT and steps[0] * (FB - 1) < (n + 1) * total_steps:
                    next(work, None)
                    steps[0] += 1
            project(*later.pop())
            t_r = None
            for t in range(TT):
                t_r = DVE.do(lambda e, t=t: e.tensor_tensor(xt[:, t, :], bank[t][:, :], xt[:, t, :], ALU.add),
                             PE.last(), t_bd[t])
                bank_free[t] = [t_r]
            t_out = d_out.start(SP, out_v[i], xt[:, :, :], t_r)

        for n in range(RING):
            fetch(n)
        for i in range(NST):
            t_sim, t_bd = attention(i)
            hidden_layers(i, t_sim, t_bd)
        for d in (d_out, d_kv, *d_save):
            SP.wait((d.sem, d.count))


_INS = ["x", "ctx_1024", "L0_xattn_Wq", "L0_xattn_bq", "L0_xattn_Wk", "L0_xattn_bk", "L0_xattn_Wv", "L0_xattn_bv",
        "L0_xattn_Wo", "L0_xattn_bo", "L0_ffn_Wg", "L0_ffn_bg", "L0_ffn_Wu", "L0_ffn_bu", "L0_ffn_Wd", "L0_ffn_bd",
        "L0_ffn_Wq", "L0_ffn_keys", "L0_ffn_down_embed", "L0_ffn_up_embed"]


def kernel(**inputs):
    import numpy as np
    import concourse.bacc as bacc
    from concourse.bass_utils import run_bass_kernel_spmd

    nc = bacc.Bacc("TRN2", target_bir_lowering=False, num_devices=1)
    arrays, args = {}, []
    for name in _INS:
        a = np.ascontiguousarray(inputs[name])
        arrays[f"in_{name}"] = a
        args.append(nc.dram_tensor(f"in_{name}", a.shape, mybir.dt.from_np(a.dtype), kind="ExternalInput").ap())
    args.append(nc.dram_tensor("out_0", (B, T, D), mybir.dt.float32, kind="ExternalOutput").ap())
    program(nc, *args)
    r = run_bass_kernel_spmd(nc, [arrays], core_ids=[0])
    return r.results[0]["out_0"]
```

```python
from contextlib import ExitStack

import concourse.bass as bass
from concourse import mybir

B, T, D = 2, 2048, 512
S, NH, E = 77, 16, 32
F = 2048
NEXP, H, NK, TOP = 2048, 4, 64, 8
P = 128
EPS = 1e-5
KD = D // P
FB = F // P
EB = NEXP // P
ST = 512
TT = ST // P
NST = B * T // ST
HG = P // E
SW = HG * S
NS = NH * S
NC = -(-NS // P)
PAIRS = [(c, g) for g in range(KD) for c in range((g * SW) // P, ((g + 1) * SW - 1) // P + 1)]
NV = len(PAIRS) * P
NX = NEXP // NK
RING = 3
ATT_PACE, RET_PACE = 1.0, 1.2
LEAD = 9
ROWS = 3 * D
SLOT = 2 * ROWS
FAR = -3.0e38


class Engine:

    def __init__(self, engine, sem):
        self.engine, self.sem, self.count, self.seen = engine, sem, 0, {}

    def wait(self, *tokens):
        for t in tokens:
            if t is None:
                continue
            sem, value = t
            if self.seen.get(id(sem), 0) < value:
                self.seen[id(sem)] = value
                self.engine.wait_ge(sem, value)

    def do(self, make, *tokens):
        self.wait(*tokens)
        self.count += 1
        make(self.engine).then_inc(self.sem, 1)
        return (self.sem, self.count)

    def quiet(self, make, *tokens):
        self.wait(*tokens)
        make(self.engine)

    def last(self):
        return (self.sem, self.count) if self.count else None


class Dma:

    def __init__(self, sem):
        self.sem, self.count = sem, 0

    def start(self, eng, out, in_, *tokens):
        eng.wait(*tokens)
        self.count += 16
        eng.engine.dma_start(out, in_).then_inc(self.sem, 16)
        return (self.sem, self.count)


def program(nc, x, ctx_in, aWq, abq, aWk, abk, aWv, abv, aWo, abo,
            Wg, bg, Wu, bu, Wd, bd, rWq, rkeys, down, up, out):
    f32, f32r, bf16 = mybir.dt.float32, mybir.dt.float32r, mybir.dt.bfloat16
    ALU, ACT, AX = mybir.AluOpType, mybir.ActivationFunctionType, mybir.AxisListType

    stack = ExitStack()
    with stack:
        def sb(name, shape, dt=f32):
            return stack.enter_context(nc.sbuf_tensor(name, shape, dt))

        def sem(name):
            return stack.enter_context(nc.semaphore(name))

        PE, DVE = Engine(nc.tensor, sem("s_tensor")), Engine(nc.vector, sem("s_vector"))
        ACTE, POOL = Engine(nc.scalar, sem("s_scalar")), Engine(nc.gpsimd, sem("s_pool"))
        SP = Engine(nc.sync, None)

        def dma(name):
            return Dma(sem(name))

        bank = [stack.enter_context(nc.psum_tensor(f"bank{i}", [P, 512], f32)) for i in range(8)]
        bank_free = [[] for _ in range(8)]

        def f(ap):
            return ap.bitcast(f32)

        def take_bank(*banks):
            for b in banks:
                PE.wait(*bank_free[b])
                bank_free[b] = []

        def mm(o, l, r, first, final, loose=False):
            PE.quiet(lambda e: e.matmul(o, l, r, start=first, stop=final, skip_group_check=loose))

        def mm_end(o, l, r, first, final, *tokens, loose=False):
            return PE.do(lambda e: e.matmul(o, l, r, start=first, stop=final, skip_group_check=loose), *tokens)

        def three(o, lH, lL, rH, rL, first, final, loose=False):
            mm(o, lH, rH, first, False, loose=loose)
            mm(o, lH, rL, False, False, loose=loose)
            return mm_end(o, lL, rH, False, final, loose=loose)

        def flip(b, col, src, *tokens, rows=P, cols=P):
            return PE.do(lambda e: e.transpose(bank[b][0:cols, col:col + rows], src, ident[0:rows, 0:rows]),
                         *tokens)

        def part(src, high, low, *tokens, col=None):
            if col is None:
                th = ACTE.do(lambda e: e.activation(high, src, ACT.Copy), *tokens)
                tl = DVE.do(lambda e: e.tensor_tensor(low, src, f(high), ALU.subtract), th)
            else:
                th = ACTE.do(lambda e: e.activation(high, src, ACT.Identity, bias=col), *tokens)
                tl = DVE.do(lambda e: e.scalar_tensor_tensor(low, src, col, f(high), ALU.add, ALU.subtract), th)
            return th, tl

        kv_dram = nc.dram_tensor("kv_scratch", (B, P, 2 * NS + 2 * NV), f32).ap()
        wq_dram = nc.dram_tensor("wq_scratch", (KD, P, 2, KD, P), f32).ap()
        wo_dram = nc.dram_tensor("wo_scratch", (P, 2 * KD * D), f32).ap()
        w2_dram = nc.dram_tensor("w2_scratch", (P, 2 * KD * D), f32).ap()
        mlp_dram = nc.dram_tensor("mlp_scratch", (FB, P, SLOT), f32).ap()
        exp_dram = nc.dram_tensor("expert_scratch", (EB, P, 4 * D), f32).ap()
        x1_dram = nc.dram_tensor("x1_scratch", (2, P, TT, D), f32).ap()

        ident = sb("ident", [P, P])
        bias_col = sb("bias_col", [P, 2 * KD + 2 * FB])
        bo_row, bd_row = sb("bo_row", [P, D]), sb("bd_row", [P, D])
        iota = sb("iota", [P, NK])
        rank_code = sb("rank_code", [P, TOP])
        t_id0 = POOL.do(lambda e: e.memset(ident[:, :], 0.0))
        t_id = POOL.do(lambda e: e.affine_select(out=ident[:, :], in_=ident[:, :], compare_op=ALU.not_equal,
                                                 fill=1.0, base=0, pattern=[[-1, P]], channel_multiplier=1), t_id0)
        POOL.do(lambda e: e.iota(iota[:, :], pattern=[[1, NK]], base=0, channel_multiplier=0,
                                 allow_small_or_imprecise_dtypes=True))
        POOL.do(lambda e: e.iota(rank_code[:, :], pattern=[[1, TOP]], base=-TOP, channel_multiplier=0,
                                 allow_small_or_imprecise_dtypes=True))

        early = ExitStack()

        def tmp(name, shape, dt=f32):
            return early.enter_context(nc.sbuf_tensor(name, shape, dt))

        d_const, d_kv, d_image = dma("s_const"), dma("s_kv"), dma("s_image")
        d_pieces, d_ctx, d_keys = dma("s_pieces"), dma("s_ctx"), dma("s_keys")
        mats = {"k": aWk, "v": aWv, "q": aWq, "o": aWo, "2": rWq}
        wraw = {n: tmp(f"raw_{n}", [P, KD, D]) for n in mats}
        d_mat = {n: dma(f"s_raw_{n}") for n in mats}
        braw = tmp("braw", [P, P])
        bv_row = tmp("bv_row", [P, D])
        craw = tmp("craw", [P, B, D])
        t_c = d_ctx.start(SP, craw[0:S, :, :], ctx_in.rearrange("b s d -> s b d"))
        t_mat = {"k": d_mat["k"].start(SP, wraw["k"][:, :, :], aWk.rearrange("(k p) n -> p k n", p=P))}
        nb = 2 * KD + 2 * FB
        at = 0
        for src, n in ((abq, KD), (abk, KD), (bg, FB), (bu, FB)):
            d_const.start(SP, braw[at:at + n, :], src.rearrange("(n p) -> n p", p=P))
            at += n
        for dst, src in ((bo_row, abo), (bd_row, bd), (bv_row, abv)):
            t_b = d_const.start(SP, dst[:, :], src.unsqueeze(0).to_broadcast([P, D]))
        for n in ("v", "q", "o", "2"):
            t_mat[n] = d_mat[n].start(SP, wraw[n][:, :, :], mats[n].rearrange("(k p) n -> p k n", p=P))
        kblk = tmp("kblk", [P, KD * P])
        keyT = tmp("keyT", [P, KD * P])
        rqT = tmp("rqT", [P, 2, KD * P])
        wkvT = tmp("wkvT", [P, 2, KD, D])
        cT = tmp("cT", [P, B, KD * S])
        vrow = tmp("vrow", [P, B, D])
        kbd = tmp("kbd", [P, NS])
        vexp = tmp("vexp", [P, NV])
        kbdH, kbdL = tmp("kbdH", [P, NS], f32r), tmp("kbdL", [P, NS], f32r)
        vexH, vexL = tmp("vexH", [P, NV], f32r), tmp("vexL", [P, NV], f32r)
        imgH, imgL = tmp("imgH", [P, KD, D], f32r), tmp("imgL", [P, KD, D], f32r)

        t_kz = DVE.do(lambda e: e.memset(kblk[:, :], 0.0))
        t_f = flip(7, 0, braw[0:nb, :], t_b, t_id, rows=nb, cols=P)
        t_bias = DVE.do(lambda e: e.tensor_copy(bias_col[:, :], bank[7][:, 0:nb]), t_f)
        bank_free[7] = [t_bias]
        bq_c = [bias_col[:, k:k + 1] for k in range(KD)]
        bk_c = [bias_col[:, KD + k:KD + k + 1] for k in range(KD)]
        bg_c = [bias_col[:, 2 * KD + k:2 * KD + k + 1] for k in range(FB)]
        bu_c = [bias_col[:, 2 * KD + FB + k:2 * KD + FB + k + 1] for k in range(FB)]
        for q in range(KD):
            for r in range(2):
                p_, h = (2 * q + r) // H, (2 * q + r) % H
                t_kp = d_keys.start(SP, kblk[r * NK:(r + 1) * NK, q * P + r * NK:q * P + (r + 1) * NK],
                                    rkeys[h, :, p_, :], t_kz)

        for w, n in enumerate(("k", "v")):
            for k in range(KD):
                take_bank(k)
                for r in range(KD):
                    t_f = flip(k, r * P, wraw[n][:, r, k * P:(k + 1) * P], t_mat[n])
                if k % 2:
                    t_w = ACTE.do(lambda e: e.activation(wkvT[:, w, k, :], bank[k][:, :], ACT.Copy), t_f)
                else:
                    t_w = t_w0 = DVE.do(lambda e: e.tensor_copy(wkvT[:, w, k, :], bank[k][:, :]), t_f)
                bank_free[k] = [t_w]
            t_wT = [t_w, t_w0]
        for b_ in range(B):
            take_bank(4)
            for k in range(KD):
                t_f = flip(4, k * S, craw[0:S, b_, k * P:(k + 1) * P], t_c, rows=S, cols=P)
            t_cT = DVE.do(lambda e: e.tensor_copy(cT[:, b_, :], bank[4][:, 0:KD * S]), t_f)
            bank_free[4] = [t_cT]
            c3 = cT[:, b_, :].rearrange("p (k n) -> p k n", k=KD)
            take_bank(5)
            PE.wait(*t_wT)
            for k in range(KD):
                t_v = mm_end(bank[5][0:S, :], c3[:, k, :], wkvT[:, 1, k, :], k == 0, k == KD - 1, t_cT)
            t_v = DVE.do(lambda e: e.tensor_tensor(vrow[0:S, b_, :], bank[5][0:S, :], bv_row[0:S, :], ALU.add), t_v, t_b)
            bank_free[5] = [t_v]
            t_z = DVE.do(lambda e: e.memset(vexp[:, :], 0.0), ACTE.last())
            for h in range(NH):
                r = h * S
                while r < (h + 1) * S:
                    c = r // P
                    n = min((h + 1) * S, (c + 1) * P) - r
                    col = PAIRS.index((c, h // HG)) * P + (h % HG) * E
                    t_p = d_pieces.start(SP, vexp[r - c * P:r - c * P + n, col:col + E],
                                         vrow[r - h * S:r - h * S + n, b_, h * E:(h + 1) * E], t_v, t_z)
                    r += n
            t_k0 = DVE.do(lambda e: e.memset(kbd[:, :], 0.0), ACTE.last())
            for g in range(KD):
                b = 6 + g % 2
                take_bank(b)
                for k in range(KD):
                    t_k = mm_end(bank[b][:, 0:S], wkvT[:, 0, k, g * P:(g + 1) * P], c3[:, k, :], k == 0, k == KD - 1)
                for r in range(HG):
                    rows = slice(r * E, (r + 1) * E)
                    col = g * SW + r * S
                    t_kb = DVE.do(lambda e: e.tensor_scalar(
                        kbd[rows, col:col + S], bank[b][rows, 0:S], bk_c[g][rows, :], None, ALU.add), t_k, t_k0)
                bank_free[b] = [t_kb]
            t_saved = (d_kv.sem, d_kv.count) if b_ else None
            DVE.wait(t_saved)
            th, tl = part(kbd[:, :], kbdH[:, :], kbdL[:, :], t_kb, t_saved)
            o = 0
            for src in (kbdH, kbdL):
                d_kv.start(SP, kv_dram[b_, :, o:o + NS], f(src[:, :]), th, tl)
                o += NS
            th, tl = part(vexp[:, :], vexH[:, :], vexL[:, :], t_p)
            for src in (vexH, vexL):
                t_kv_saved = d_kv.start(SP, kv_dram[b_, :, o:o + NV], f(src[:, :]), th, tl)
                o += NV

        take_bank(4)
        for q in range(KD):
            t_f = flip(4, q * P, kblk[:, q * P:(q + 1) * P], t_kp)
        t_keyT = DVE.do(lambda e: e.tensor_copy(keyT[:, :], bank[4][:, :]), t_f)
        bank_free[4] = [t_keyT]
        t_image = None
        for n in ("q", "o", "2"):
            DVE.wait(t_image)
            ACTE.wait(t_image)
            for k in range(KD):
                b = k
                take_bank(b)
                if n != "2":
                    for r in range(KD):
                        t_f = flip(b, r * P, wraw[n][:, r, k * P:(k + 1) * P], t_mat[n])
                else:
                    bb = 4 + k % 2
                    take_bank(bb)
                    for q in range(KD):
                        t_f = flip(bb, q * P, wraw[n][:, k, q * P:(q + 1) * P], t_mat[n])
                    t_r = DVE.do(lambda e: e.tensor_copy(rqT[:, k % 2, :], bank[bb][:, :]), t_f)
                    bank_free[bb] = [t_r]
                    for q in range(KD):
                        c = slice(q * P, (q + 1) * P)
                        t_f = mm_end(bank[b][:, c], rqT[:, k % 2, c], keyT[:, c], True, True, t_r, t_keyT)
                th, tl = part(bank[b][:, :], imgH[:, k, :], imgL[:, k, :], t_f)
                bank_free[b] = [th, tl]
            for i, src in enumerate((imgH, imgL)):
                if n == "q":
                    for g in range(KD):
                        t_image = d_image.start(SP, wq_dram[g, :, i, :, :], f(src[:, :, g * P:(g + 1) * P]), th, tl)
                else:
                    dst = wo_dram if n == "o" else w2_dram
                    t_image = d_image.start(SP, dst[:, i * KD * D:(i + 1) * KD * D],
                                            f(src[:, :, :]).rearrange("p k n -> p (k n)"), th, tl)
        everyone = [PE.last(), DVE.last(), ACTE.last(), POOL.last(), t_image, t_kv_saved]
        for e in (PE, DVE, ACTE, POOL, SP):
            e.wait(*everyone)
        early.close()

        ROOM = [2 * KD * ST, 2 * KD * ST, 4 * ST]
        with ExitStack() as plain:
            z_plain0, z_plain1, narrow_plain = (
                plain.enter_context(nc.sbuf_tensor(f"plain{i}", [P, n], f32)) for i, n in enumerate(ROOM))
        z_plain = [z_plain0, z_plain1]
        z_room = [sb(f"zT{i}", [P, ROOM[i]], f32r) for i in range(2)]
        narrow = sb("narrow", [P, ROOM[2]], f32r)
        ring = [sb(f"ring{i}", [P, SLOT], f32r) for i in range(RING)]
        raw = [sb(f"raw{i}", [P, D]) for i in range(2)]
        keysH, keysL = sb("keysH", [P, NS], f32r), sb("keysL", [P, NS], f32r)
        valsH, valsL = sb("valsH", [P, NV], f32r), sb("valsL", [P, NV], f32r)
        xt = sb("xt", [P, TT, D])
        zTs = [tuple(z[:, o:o + KD * ST].rearrange("p (k t) -> p k t", k=KD) for o in (0, KD * ST)) for z in z_room]
        wide = sb("wide", [P, 2 * KD * ST], f32r)
        qH = wide[:, 0:KD * ST].rearrange("p (k t) -> p k t", k=KD)
        qL = wide[:, KD * ST:2 * KD * ST].rearrange("p (k t) -> p k t", k=KD)
        turned = [(narrow[:, 2 * c * ST:(2 * c + 1) * ST], narrow[:, (2 * c + 1) * ST:(2 * c + 2) * ST]) for c in range(2)]
        sims = [narrow_plain[:, t * D:(t + 1) * D] for t in range(TT)]
        last_probs = sb("last_probs", [P, NS])
        zn = sb("zn", [P, D])
        result = [sb(f"result{i}", [P, D]) for i in range(2)] + raw
        gate = [sb(f"gate{i}", [P, ST]) for i in range(2)]
        hidH = [sb(f"hid{i}H", [P, ST], f32r) for i in range(2)]
        hidL = [sb(f"hid{i}L", [P, ST], f32r) for i in range(2)]
        dense = [sb(f"dense{i}", [P, TT * P]) for i in range(2)]
        kept = [sb(f"kept{i}", [P, TT * P], bf16) for i in range(H)]
        spreadV, spreadG = sb("spreadV", [P, TT * P]), sb("spreadG", [P, TT * P])
        firsts = [sb(f"firsts{i}", [P, TT, H * NX]) for i in range(2)]
        seconds = [sb(f"seconds{i}", [P, TT, H * NK]) for i in range(2)]
        counts = [sb(f"counts{i}", [P, TT, H * NX], bf16) for i in range(2)]
        codes = [sb(f"codes{i}", [P, TT, H * NK], bf16) for i in range(2)]
        clamps = sb("clamps", [P, 2, TT])
        stats = sb("stats", [P, 2, 6])
        mv = sb("mv", [P, TT, 2])
        std, rstd = sb("std", [P, TT]), sb("rstd", [P, TT])
        mx, den, rden = (sb(n, [P, NH]) for n in ("mx", "den", "rden"))
        HT, HC = H * TOP, H * TOP * TOP
        top = sb("top", [P, 2 * HT])
        index = sb("index", [P, 2 * HT], mybir.dt.uint32)
        index_f = sb("index_f", [P, 2 * HT])
        cand = sb("cand", [P, HC])
        left = sb("left", [P, HC])
        weight = sb("weight", [P, HC])
        best, count, row, beyond = (sb(n, [P, HT]) for n in ("best", "count", "row", "beyond"))
        total, inv = sb("total", [P, H]), sb("inv", [P, H])
        onehot = sb("onehot", [P, H * TOP * NK // 2], bf16)

        NB = FB + EB
        MLP, EXPERT = 0, 1
        pairs = [(kind, j) for j in range(FB) for kind in (MLP, EXPERT)]
        lead = [(MLP, j) for j in range(LEAD)]
        for j in range(EB):
            lead += [(EXPERT, j)] + ([(MLP, j + LEAD)] if j + LEAD < FB else [])
        order = lead + pairs * (NST - 1)
        d_ring = [dma(f"s_ring{i}") for i in range(RING)]
        d_save = [dma(f"s_save{i}") for i in range(RING)]
        d_raw = [dma(f"s_raw{i}") for i in range(2)]
        slot_ready, slot_free, t_written, made = {}, [None] * RING, {}, {}
        raw_free, raw_sent, raw_used = [[], []], [], [0]
        raw_order = []
        for kind, m in lead:
            cols = slice(m * P, (m + 1) * P)
            if kind == MLP:
                for W in (Wg, Wu):
                    raw_order.append((lambda r: r[:, :].rearrange("p (k n) -> p k n", k=KD),
                                      W[:, cols].rearrange("(k p) n -> p k n", p=P)))
            for W in (Wd,) if kind == MLP else (down, up):
                raw_order.append((lambda r: r[:, :], W[cols, :]))

        def send_raw():
            n = len(raw_sent)
            if n < len(raw_order):
                dst, src = raw_order[n]
                raw_sent.append(d_raw[n % 2].start(SP, dst(raw[n % 2]), src, *raw_free[n % 2]))

        def make_slot(n):
            s = n % RING
            mlp, j = order[n][0] == MLP, order[n][1]
            words = 3 * D if mlp else 2 * D
            tokens = []
            for c in range(3 if mlp else 2):
                r = raw_used[0]
                raw_used[0] += 1
                hi = ring[s][:, c * D:(c + 1) * D]
                lo = ring[s][:, words + c * D:words + (c + 1) * D]
                free = [slot_free[s], made.get(n - RING)]
                DVE.wait(*free)
                if not mlp and c == 0:
                    b = 5
                    take_bank(b)
                    for k in range(KD):
                        t_f = flip(b, k * P, raw[r % 2][:, k * P:(k + 1) * P], raw_sent[r])
                    th, tl = part(bank[b][:, :], hi, lo, t_f, *free)
                    bank_free[b] = [th, tl]
                    raw_free[r % 2] = [t_f]
                else:
                    th, tl = part(raw[r % 2][:, :], hi, lo, raw_sent[r], *free)
                    raw_free[r % 2] = [th, tl]
                tokens += [th, tl]
                send_raw()
            slot_ready[n] = tokens
            dst = mlp_dram[j] if mlp else exp_dram[j]
            t_written[order[n]] = made[n] = d_save[s].start(SP, dst, f(ring[s][:, 0:2 * words]), *tokens)

        def fill_slot(n):
            if n >= NB * NST:
                return
            if n < NB:
                make_slot(n)
                return
            s = n % RING
            mlp, j = order[n][0] == MLP, order[n][1]
            src = mlp_dram[j] if mlp else exp_dram[j]
            slot_ready[n] = [d_ring[s].start(SP, f(ring[s][:, 0:(6 if mlp else 4) * D]), src,
                                             slot_free[s], t_written[order[n]], made.get(n - RING))]

        x_v = x.rearrange("b (s t p) d -> (b s) p t d", t=TT, p=P)
        out_v = out.rearrange("b (s t p) d -> (b s) p t d", t=TT, p=P)
        d_x, d_x1 = dma("s_x"), dma("s_x1")
        d_wq = [dma(f"s_wq{i}") for i in range(2)]
        d_wide = dma("s_wide")
        d_res = [dma(f"s_res{i}") for i in range(TT)]
        d_out = [dma(f"s_out{i}") for i in range(TT)]
        x_sent, x1_saved, retrieved, spread_done = {}, {}, {}, {}

        stats_used, zn_used = [[], []], [None, None]

        def statistics(t, *tokens):
            ts = DVE.do(lambda e: e.bn_stats(stats[:, t % 2, :], xt[:, t, :]), *tokens, *stats_used[t % 2])
            tm = DVE.do(lambda e: e.bn_aggr(mv[:, t, :], stats[:, t % 2, :]), ts, zn_used[0])
            stats_used[t % 2] = [tm]
            return tm

        def normalise(zT, tm, t_z, row, t_row):
            te = DVE.do(lambda e: e.tensor_scalar(std[:, :], mv[:, :, 1], EPS, None, ALU.add), tm, zn_used[0])
            tq = ACTE.do(lambda e: e.activation(std[:, :], std[:, :], ACT.Sqrt), te)
            yield
            t_std = DVE.do(lambda e: e.reciprocal(rstd[:, :], std[:, :]), tq)

            def centre(t):
                tz = zn_used[0] = DVE.do(lambda e: e.tensor_scalar(
                    zn[:, :], xt[:, t, :], mv[:, t, 0:1], rstd[:, t:t + 1], ALU.subtract, ALU.mult), t_std, zn_used[1])
                t_row.append(POOL.do(lambda e: e.tensor_tensor(xt[:, t, :], xt[:, t, :], row[:, :], ALU.add), tz))
                return tz

            tz = centre(0)
            yield
            for t in range(TT):
                b = 6 + t % 2
                take_bank(b)
                for k in range(KD):
                    zn_used[1] = flip(b, k * P, zn[:, k * P:(k + 1) * P], tz)
                tok = slice(t * P, (t + 1) * P)
                src = bank[b][:, :].rearrange("p (k t) -> p k t", k=KD)
                th, tl = part(src, zT[0][:, :, tok], zT[1][:, :, tok], zn_used[1])
                bank_free[b] = [th, tl]
                t_z.append([th, tl])
                if t + 1 < TT:
                    tz = centre(t + 1)
                yield

        def send_x(i):
            x_sent[i] = d_x.start(SP, xt[:, :, :], x_v[i], x1_saved.get(i - 1), zn_used[0])

        def attention(i):
            zT = zTs[i % 2]
            t_x = x_sent.pop(i)
            if i % (NST // B) == 0:
                o = 0
                for dst, n in ((keysH, NS), (keysL, NS), (valsH, NV), (valsL, NV)):
                    d_kv.start(SP, f(dst[:, :]), kv_dram[i // (NST // B), :, o:o + n], PE.last())
                    o += n
            t_kv = (d_kv.sem, d_kv.count)

            def send_wq(g):
                c = (g % 2) * 2 * KD * P
                return d_wq[g % 2].start(SP, f(narrow[:, c:c + 2 * KD * P]),
                                         wq_dram[g].rearrange("p a k n -> p (a k n)"), PE.last(), sims_taken[0])

            t_wq = {g: send_wq(g) for g in range(2)}
            yield
            for t in range(TT):
                tm = statistics(t, t_x)
                if t % 2:
                    yield
            t_bo, t_z = [], []
            for _ in normalise(zT, tm, t_z, bo_row, t_bo):
                yield
            t_z = t_z[-1]
            for g in range(KD):
                b = 6 + g % 2
                take_bank(b)
                PE.wait(*t_z, t_wq[g])
                c = (g % 2) * 2 * KD * P
                for k in range(KD):
                    w = narrow[:, c + k * P:c + (k + 1) * P]
                    w_ = narrow[:, c + (KD + k) * P:c + (KD + k + 1) * P]
                    t_q = three(bank[b][:, :], w, w_, zT[0][:, k, :], zT[1][:, k, :], k == 0, k == KD - 1)
                th, tl = part(bank[b][:, :], qH[:, g, :], qL[:, g, :], t_q, col=bq_c[g])
                bank_free[b] = [th, tl]
                t_qs = [th, tl]
                if g + 2 < KD:
                    t_wq[g + 2] = send_wq(g + 2)
                yield

            probs = [z_plain[i % 2][:, t * NS:(t + 1) * NS] for t in range(TT - 1)] + [last_probs[:, :]]

            def scores(t, half):
                tok = slice(t * P, (t + 1) * P)
                for g in (2 * half, 2 * half + 1):
                    b = 6 + g % 2
                    take_bank(b)
                    PE.wait(*t_qs, t_kv)
                    c = slice(g * SW, (g + 1) * SW)
                    t_s = three(bank[b][:, 0:SW], qH[:, g, tok], qL[:, g, tok], keysH[:, c], keysL[:, c], True, True)
                    v = bank[b][:, 0:SW].rearrange("p (h s) -> p h s", h=HG)
                    hs = slice(g * HG, (g + 1) * HG)
                    t_m = DVE.do(lambda e: e.tensor_reduce(mx[:, hs], v, AX.X, ALU.max), t_s, mx_used[0])
                    mx_used[0] = t_d = DVE.do(lambda e: e.tensor_tensor(
                        probs[t][:, c].rearrange("p (h s) -> p h s", h=HG), v,
                        mx[:, hs].unsqueeze(2).to_broadcast([P, HG, S]), ALU.subtract), t_m)
                    bank_free[b] = [t_d]
                return t_d

            def weigh(t, t_d):
                p3 = probs[t].rearrange("p (h s) -> p h s", h=NH)
                t_e = ACTE.do(lambda e: e.activation(probs[t], probs[t], ACT.Exp, scale=E ** -0.5), t_d)
                yield
                t_n = DVE.do(lambda e: e.tensor_reduce(den[:, :], p3, AX.X, ALU.add), t_e, rden_used[0])
                t_r = DVE.do(lambda e: e.reciprocal(rden[:, :], den[:, :]), t_n)
                rden_used[0] = POOL.do(lambda e: e.tensor_tensor(
                    p3, p3, rden[:, :].unsqueeze(2).to_broadcast([P, NH, S]), ALU.mult), t_r)
                t_probs.append(rden_used[0])

            t_probs, weighing = [], iter(())
            for t in range(TT):
                scores(t, 0)
                next(weighing, None)
                yield
                t_d = scores(t, 1)
                weighing = weigh(t, t_d)
                next(weighing)
                yield
            next(weighing, None)
            yield

            def turn(c):
                n = min(P, NS - c * P)
                take_bank(7)
                for t in range(TT):
                    t_f = flip(7, t * P, probs[t][:, c * P:c * P + n], t_probs[t], cols=n)
                hi, lo = turned[c % 2]
                th, tl = part(bank[7][0:n, :], hi[0:n, :], lo[0:n, :], t_f)
                bank_free[7] = [th, tl]
                return [th, tl]

            yield
            t_turned = {0: turn(0)}
            t_att = {}
            for m, (c, g) in enumerate(PAIRS):
                yield
                if c + 1 < NC and c + 1 not in t_turned:
                    t_turned[c + 1] = turn(c + 1)
                first, final = m == 0 or PAIRS[m - 1][1] != g, m + 1 == len(PAIRS) or PAIRS[m + 1][1] != g
                if first:
                    take_bank(6)
                PE.wait(*t_turned[c])
                n = min(P, NS - c * P)
                v = slice(m * P, (m + 1) * P)
                hi, lo = turned[c % 2]
                t_o = three(bank[6][:, :], valsH[0:n, v], valsL[0:n, v], hi[0:n, :], lo[0:n, :], first, final)
                if final:
                    t_att[g] = part(bank[6][:, :], qH[:, g, :], qL[:, g, :], t_o)
                    bank_free[6] = [*t_att[g]]
            wo = z_room[i % 2]
            t_w = d_wide.start(SP, f(wo[:, :]), wo_dram, PE.last())
            yield
            yield
            yield
            for t in range(TT):
                tok = slice(t * P, (t + 1) * P)
                b = 6 + t % 2
                take_bank(b)
                PE.wait(*t_att[KD - 1], t_w)
                for k in range(KD):
                    t_y = three(bank[b][:, :], qH[:, k, tok], qL[:, k, tok], wo[:, k * D:(k + 1) * D],
                                wo[:, (KD + k) * D:(KD + k + 1) * D], k == 0, k == KD - 1)
                t_x1 = DVE.do(lambda e: e.tensor_tensor(xt[:, t, :], bank[b][:, :], xt[:, t, :], ALU.add), t_y, t_bo[t])
                bank_free[b] = [t_x1]
                tm = statistics(t, t_x1)
                yield
            t_w = d_wide.start(SP, f(wide[:, :]), w2_dram, PE.last())
            t_z2, t_bd = [], []
            for _ in normalise(zT, tm, t_z2, bd_row, t_bd):
                yield
            t_sim = []
            for t in range(TT):
                tok = slice(t * P, (t + 1) * P)
                b = 6 + t % 2
                take_bank(b)
                PE.wait(*t_z2[t], t_w)
                for k in range(KD):
                    t_y = three(bank[b][:, :], zT[0][:, k, tok], zT[1][:, k, tok], wide[:, k * D:(k + 1) * D],
                                wide[:, (KD + k) * D:(KD + k + 1) * D], k == 0, k == KD - 1)
                t_c = ACTE.do(lambda e: e.activation(sims[t], bank[b][:, :], ACT.Copy), t_y)
                bank_free[b] = [t_c]
                t_sim.append(t_c)
                yield
            x1_saved[i] = d_x1.start(SP, x1_dram[i % 2], xt[:, :, :], *t_bd)
            attended[i] = (t_sim, t_z2)

        mx_used, rden_used = [None], [None]
        attended, sims_taken = {}, [None]

        def retrieval(i, t):
            V = DVE.do
            i_ = i % 2
            first, second = firsts[i_][:, t, :], seconds[i_][:, t, :]
            code, row_n = codes[i_][:, t, :], counts[i_][:, t, :]
            t_sim = attended[i][0][t]
            sim = sims[t].rearrange("p (g n) -> p g n", g=2 * H)
            top3 = top[:, :].rearrange("p (g n) -> p g n", g=2 * H)
            for half in range(2):
                gs = range(half * H, (half + 1) * H)
                for g in gs:
                    t1 = V(lambda e: e.max(top3[:, g, :], sim[:, g, :]), t_sim)
                for g in gs:
                    t1 = V(lambda e: e.max_index(index[:, g * TOP:(g + 1) * TOP], top3[:, g, :], sim[:, g, :]), t1)
                yield
            t1 = V(lambda e: e.tensor_copy(index_f[:, :], index[:, :]), t1)
            t5 = V(lambda e: e.tensor_tensor(
                first.rearrange("p (h n) -> p h n", h=H), sim[:, 0:H, 0:NX],
                top3[:, 0:H, 0:1].to_broadcast([P, H, NX]), ALU.subtract), t1, *spread_done.get(i - 2, []))
            t5 = V(lambda e: e.tensor_tensor(
                second.rearrange("p (h n) -> p h n", h=H), sim[:, H:2 * H, :],
                top3[:, H:2 * H, 0:1].to_broadcast([P, H, NK]), ALU.subtract), t5)
            c4 = cand[:, :].rearrange("p (h a b) -> p h a b", h=H, a=TOP)
            for h in range(H):
                t2 = V(lambda e: e.tensor_tensor(
                    c4[:, h, :, :], top3[:, h, :].unsqueeze(2).to_broadcast([P, TOP, TOP]),
                    top3[:, H + h, :].unsqueeze(1).to_broadcast([P, TOP, TOP]), ALU.add), t1)
            c2 = cand[:, :].rearrange("p (h n) -> p h n", h=H)
            l2 = left[:, :].rearrange("p (h n) -> p h n", h=H)
            b2 = best[:, :].rearrange("p (h n) -> p h n", h=H)
            for h in range(H):
                t3 = V(lambda e: e.max(b2[:, h, :], c2[:, h, :]), t2)
            yield
            for h in range(H):
                t3 = V(lambda e: e.match_replace(l2[:, h, :], b2[:, h, :], c2[:, h, :], FAR), t3)
            t4 = V(lambda e: e.tensor_tensor(weight[:, :].rearrange("p (h n) -> p h n", h=H), c2,
                                             b2[:, :, 0:1].to_broadcast([P, H, TOP * TOP]), ALU.subtract), t3)
            t4 = ACTE.do(lambda e: e.activation(weight[:, :], weight[:, :], ACT.Exp), t4)
            ta = ACTE.do(lambda e: e.activation(first, first, ACT.Exp), t5)
            tb = ACTE.do(lambda e: e.activation(second, second, ACT.Exp), t5)
            yield
            t3 = V(lambda e: e.tensor_tensor(left[:, :], left[:, :], cand[:, :], ALU.is_lt), t3)
            t_n = V(lambda e: e.tensor_reduce(count[:, :], left[:, :].rearrange("p (r n) -> p r n", n=TOP), AX.X, ALU.add), t3)
            oh = onehot[:, 0:H * TOP * NX].rearrange("p (h r i) -> p h r i", h=H, r=TOP)
            for h in range(H):
                t9 = V(lambda e: e.tensor_tensor(
                    oh[:, h], iota[:, 0:NX].unsqueeze(1).to_broadcast([P, TOP, NX]),
                    index_f[:, h * TOP:(h + 1) * TOP].unsqueeze(2).to_broadcast([P, TOP, NX]), ALU.is_equal), t1)
                if h % 2:
                    yield
            of = onehot[:, 0:H * TOP * NX].rearrange("p (m i) -> p m i", i=NX)
            t9 = V(lambda e: e.tensor_tensor(of, of, count[:, :].unsqueeze(2).to_broadcast([P, HT, NX]), ALU.mult), t9, t_n)
            t9 = fold(oh, NX, row_n, t9)
            yield
            t4 = V(lambda e: e.tensor_tensor(weight[:, :], weight[:, :], left[:, :], ALU.mult), t4, t3)
            t4 = V(lambda e: e.tensor_reduce(row[:, :], weight[:, :].rearrange("p (r n) -> p r n", n=TOP), AX.X, ALU.add), t4)
            t6 = V(lambda e: e.tensor_reduce(total[:, :], row[:, :].rearrange("p (h n) -> p h n", h=H), AX.X, ALU.add), t4)
            t6 = V(lambda e: e.reciprocal(inv[:, :], total[:, :]), t6)
            t8 = V(lambda e: e.tensor_tensor(first.rearrange("p (h n) -> p h n", h=H), first.rearrange("p (h n) -> p h n", h=H),
                                             inv[:, :].unsqueeze(2).to_broadcast([P, H, NX]), ALU.mult), ta, t6)
            t7 = V(lambda e: e.scalar_tensor_tensor(beyond[:, :], index_f[:, 0:HT], float(NX), row[:, :],
                                                    ALU.is_ge, ALU.mult), t6)
            b3 = beyond[:, :].rearrange("p (h n) -> p h n", h=H)
            t7 = V(lambda e: e.tensor_tensor(b3, b3, inv[:, :].unsqueeze(2).to_broadcast([P, H, TOP]), ALU.mult), t7)
            t7 = V(lambda e: e.tensor_reduce(clamps[:, i_, t:t + 1], beyond[:, :], AX.X, ALU.add), t7)
            yield
            oh = onehot[:, :].rearrange("p (h r i) -> p h r i", h=H // 2, r=TOP)
            tc = t9
            for pair in range(2):
                for r in range(H // 2):
                    c = HT + (pair * H // 2 + r) * TOP
                    tc = V(lambda e: e.tensor_tensor(
                        oh[:, r], iota[:, :].unsqueeze(1).to_broadcast([P, TOP, NK]),
                        index_f[:, c:c + TOP].unsqueeze(2).to_broadcast([P, TOP, NK]), ALU.is_equal), tc)
                yield
                for r in range(H // 2):
                    tc = V(lambda e: e.tensor_tensor(
                        oh[:, r], oh[:, r], rank_code[:, :].unsqueeze(2).to_broadcast([P, TOP, NK]), ALU.mult), tc)
                yield
                tc = fold(oh, NK, code[:, pair * (H // 2) * NK:(pair + 1) * (H // 2) * NK], tc)
            tc = V(lambda e: e.tensor_scalar(code, code, float(TOP), None, ALU.add), tc)
            sims_taken[0] = tc
            retrieved[i] = retrieved.get(i, []) + [tc, t8, t7, tb]
            yield

        def fold(oh, n, dst, token):
            for m in (4, 2):
                token = DVE.do(lambda e: e.tensor_tensor(
                    oh[:, :, 0:m, :].rearrange("p h r i -> p h (r i)"), oh[:, :, 0:m, :].rearrange("p h r i -> p h (r i)"),
                    oh[:, :, m:2 * m, :].rearrange("p h r i -> p h (r i)"), ALU.add), token)
            return DVE.do(lambda e: e.tensor_tensor(dst.rearrange("p (h i) -> p h i", i=n),
                                                    oh[:, :, 0, :], oh[:, :, 1, :], ALU.add), token)

        dense_ready, dense_free = {}, [None, None]
        kept_free = [None] * H
        IB = P // NK

        def spread(i, eb):
            i_ = i % 2
            d4 = dense[eb % 2][:, :].rearrange("p (t i j) -> p t i j", t=TT, i=IB)

            def by_first(a, h):
                o = h * NX + eb * IB
                return a[i_][:, :, o:o + IB].unsqueeze(3).to_broadcast([P, TT, IB, NK])

            def by_second(a, h):
                return a[i_][:, :, h * NK:(h + 1) * NK].unsqueeze(2).to_broadcast([P, TT, IB, NK])

            def shaped(a):
                return a[:, :].rearrange("p (t i j) -> p t i j", t=TT, i=IB)

            kp = POOL.last()
            for h in range(H):
                k4 = shaped(kept[h])
                k = DVE.do(lambda e: e.tensor_tensor(k4, by_second(codes, h), by_first(counts, h), ALU.is_lt),
                           *retrieved[i], kept_free[h])
                yield
                if h == 0:
                    v4 = shaped(spreadV)
                    k = DVE.do(lambda e: e.tensor_tensor(v4, k4, by_first(firsts, h), ALU.mult), k)
                    kept_free[h] = k
                    yield
                    k = k0 = DVE.do(lambda e: e.tensor_tensor(d4, v4, by_second(seconds, h), ALU.mult), k, dense_free[eb % 2])
                    if eb == EB - 1:
                        last = d4[:, :, IB - 1, NK - 1]
                        k0 = DVE.do(lambda e: e.tensor_tensor(last, last, clamps[:, i_, :], ALU.add), k)
                    yield
                else:
                    g4 = shaped(spreadG)
                    kp = POOL.do(lambda e: e.tensor_tensor(g4, k4, by_first(firsts, h), ALU.mult), k, kp)
                    kept_free[h] = kp
                    kp = POOL.do(lambda e: e.tensor_tensor(g4, g4, by_second(seconds, h), ALU.mult), kp)
                    kp = POOL.do(lambda e: e.tensor_tensor(d4, d4, g4, ALU.add), kp, k0)
            dense_ready[i, eb] = kp
            if eb == EB - 1:
                spread_done[i] = [kp, DVE.last()]

        def all_weights():
            for i in range(NST):
                for eb in range(EB):
                    while experts_done[0] < i * EB + eb - 1 or len(retrieved.get(i, [])) < 4 * TT:
                        yield
                    for _ in spread(i, eb):
                        yield

        def background():
            for t in range(TT):
                for _ in retrieval(0, t):
                    yield 0.5
            for i in range(1, NST):
                for _ in attention(i):
                    yield ATT_PACE if i > 1 else 0.85
                for t in range(TT):
                    for _ in retrieval(i, t):
                        yield RET_PACE if i > 1 else 0.9
                    if t == 0 and i + 1 < NST:
                        send_x(i + 1)
                while current[0] < i:
                    yield 1.0

        for _ in range(2):
            send_raw()
        send_x(0)
        for n in range(RING):
            fill_slot(n)
        for _ in attention(0):
            pass
        send_x(1)

        def project(i, n, m, wH, wL, ready):
            nb_ = n % NB
            if nb_ == 0:
                take_bank(*range(TT))
            PE.wait(*ready)
            for t in range(TT):
                tok = slice(t * P, (t + 1) * P)
                k = three(bank[t][:, :], hidH[m][:, tok], hidL[m][:, tok], wH, wL, nb_ == 0, nb_ == NB - 1)
            slot_free[n % RING] = k
            fill_slot(n + RING)
            if nb_ == NB - 1:
                finish(i, k)

        def send_back(i):
            for t in range(TT):
                t_back[t] = d_res[t].start(SP, result[t][:, :], x1_dram[i % 2, :, t, :], x1_saved[i],
                                           (d_out[t].sem, d_out[t].count), *(raw_free[t - 2] if t >= 2 else ()))

        def finish(i, k):
            for t in range(TT):
                r = result[t]
                t_r = DVE.do(lambda e: e.tensor_tensor(r[:, :], bank[t][:, :], r[:, :], ALU.add), k, t_back[t])
                bank_free[t] = [t_r]
                d_out[t].start(SP, out_v[i][:, t, :], r[:, :], t_r)

        t_back = [None] * TT
        experts_done, current, spent = [0], [0], [0.0]
        weights, beside = all_weights(), background()

        def aside():
            next(weights, None)
            spent[0] -= 1.0
            while spent[0] < 0.0:
                spent[0] += next(beside, 1.0)

        later = None
        for n in range(NST * NB):
            i, nb_ = n // NB, n % NB
            kind, j = order[n]
            m = n % 2
            zT = zTs[i % 2]
            w = ring[n % RING]
            if nb_ == 0:
                current[0] = i
                while i not in attended:
                    next(beside)
                PE.wait(*(tok for z in attended[i][1] for tok in z))
            if nb_ == NB - 1:
                send_back(i)
            take_bank(4)
            PE.wait(*slot_ready.pop(n))
            words = (3 if kind == MLP else 2) * D
            for k in range(KD):
                c = k * P
                t_g0 = three(bank[4][:, :], w[:, c:c + P], w[:, words + c:words + c + P],
                             zT[0][:, k, :], zT[1][:, k, :], k == 0, k == KD - 1)
            if kind == MLP:
                t_s = ACTE.do(lambda e: e.activation(gate[m][:, :], bank[4][:, :], ACT.Silu, bias=bg_c[j]), t_g0)
                aside()
                take_bank(5)
                for k in range(KD):
                    c = D + k * P
                    t_g = three(bank[5][:, :], w[:, c:c + P], w[:, words + c:words + c + P],
                                zT[0][:, k, :], zT[1][:, k, :], k == 0, k == KD - 1)
                t_h = DVE.do(lambda e: e.scalar_tensor_tensor(gate[m][:, :], bank[5][:, :], bu_c[j], gate[m][:, :],
                                                              ALU.add, ALU.mult), t_g, t_s)
            else:
                t_s = ACTE.do(lambda e: e.activation(gate[m][:, :], bank[4][:, :], ACT.Silu), t_g0)
                aside()
                while (i, j) not in dense_ready:
                    next(weights)
                take_bank(5)
                for t in range(TT):
                    t_g = flip(5, t * P, dense[j % 2][:, t * P:(t + 1) * P], dense_ready[i, j])
                dense_free[j % 2] = t_g
                experts_done[0] += 1
                t_h = DVE.do(lambda e: e.tensor_tensor(gate[m][:, :], bank[5][:, :], gate[m][:, :], ALU.mult), t_g, t_s)
            bank_free[4], bank_free[5] = [t_s], [t_h]
            t_hi = ACTE.do(lambda e: e.activation(hidH[m][:, :], gate[m][:, :], ACT.Copy), t_h)
            aside()
            t_lo = DVE.do(lambda e: e.tensor_tensor(hidL[m][:, :], gate[m][:, :], f(hidH[m][:, :]), ALU.subtract), t_hi)
            ready = (t_hi, t_lo)
            if later:
                project(*later)
            aside()
            o = words - D
            later = (i, n, m, w[:, o:o + D], w[:, words + o:words + o + D], ready)
            aside()
        project(*later)
        for d in (*d_out, *d_save, d_kv, d_image, d_x1):
            SP.wait((d.sem, d.count))


_INS = ["x", "ctx_1024", "L0_xattn_Wq", "L0_xattn_bq", "L0_xattn_Wk", "L0_xattn_bk", "L0_xattn_Wv", "L0_xattn_bv",
        "L0_xattn_Wo", "L0_xattn_bo", "L0_ffn_Wg", "L0_ffn_bg", "L0_ffn_Wu", "L0_ffn_bu", "L0_ffn_Wd", "L0_ffn_bd",
        "L0_ffn_Wq", "L0_ffn_keys", "L0_ffn_down_embed", "L0_ffn_up_embed"]


def kernel(**inputs):
    import numpy as np
    import concourse.bacc as bacc
    from concourse.bass_utils import run_bass_kernel_spmd

    nc = bacc.Bacc("TRN2", target_bir_lowering=False, num_devices=1)
    arrays, args = {}, []
    for name in _INS:
        a = np.ascontiguousarray(inputs[name])
        arrays[f"in_{name}"] = a
        args.append(nc.dram_tensor(f"in_{name}", a.shape, mybir.dt.from_np(a.dtype), kind="ExternalInput").ap())
    args.append(nc.dram_tensor("out_0", (B, T, D), mybir.dt.float32, kind="ExternalOutput").ap())
    program(nc, *args)
    r = run_bass_kernel_spmd(nc, [arrays], core_ids=[0])
    return r.results[0]["out_0"]
```

```python
import math
from contextlib import ExitStack

import concourse.bass as bass
from concourse import mybir

B, T, D = 2, 2048, 512
S, NH, E = 77, 16, 32
F = 2048
NEXP, H, NK, TOP = 2048, 4, 64, 8
P = 128
EPS = 1e-5
KD = D // P
FB = F // P
EB = NEXP // P
IB = P // NK
ST = 512
TT = ST // P
NST = B * T // ST
HG = P // E
SW = HG * S
NS = NH * S
NC = -(-NS // P)
PAIRS = [(c, g) for g in range(KD) for c in range((g * SW) // P, ((g + 1) * SW - 1) // P + 1)]
NV = len(PAIRS) * P
NX = NEXP // NK
RING = 3
ATT_PACE, RET_PACE = 1.0, 1.35
MIX = "MM" + 5 * "EEM" + 3 * "MME" + 3 * "ME"
LEAD = 8
SECOND = 4 * D
SLOT = SECOND + 2 * D
FAR = -3.0e38


class Engine:

    def __init__(self, engine, sem):
        self.engine, self.sem, self.count, self.seen = engine, sem, 0, {}

    def wait(self, *tokens):
        for t in tokens:
            if t is None:
                continue
            sem, value = t
            if self.seen.get(id(sem), 0) < value:
                self.seen[id(sem)] = value
                self.engine.wait_ge(sem, value)

    def do(self, make, *tokens):
        self.wait(*tokens)
        self.count += 1
        make(self.engine).then_inc(self.sem, 1)
        return (self.sem, self.count)

    def quiet(self, make, *tokens):
        self.wait(*tokens)
        make(self.engine)

    def last(self):
        return (self.sem, self.count) if self.count else None


class Dma:

    def __init__(self, sem):
        self.sem, self.count = sem, 0

    def start(self, eng, out, in_, *tokens):
        eng.wait(*tokens)
        self.count += 16
        eng.engine.dma_start(out, in_).then_inc(self.sem, 16)
        return (self.sem, self.count)


def program(nc, x, ctx_in, aWq, abq, aWk, abk, aWv, abv, aWo, abo,
            Wg, bg, Wu, bu, Wd, bd, rWq, rkeys, down, up, out):
    f32, f32r, bf16 = mybir.dt.float32, mybir.dt.float32r, mybir.dt.bfloat16
    ALU, ACT, AX = mybir.AluOpType, mybir.ActivationFunctionType, mybir.AxisListType

    stack = ExitStack()
    with stack:
        def sb(name, shape, dt=f32):
            return stack.enter_context(nc.sbuf_tensor(name, shape, dt))

        def sem(name):
            return stack.enter_context(nc.semaphore(name))

        PE, DVE = Engine(nc.tensor, sem("s_tensor")), Engine(nc.vector, sem("s_vector"))
        ACTE, POOL = Engine(nc.scalar, sem("s_scalar")), Engine(nc.gpsimd, sem("s_pool"))
        SP = Engine(nc.sync, None)

        def dma(name):
            return Dma(sem(name))

        bank = [stack.enter_context(nc.psum_tensor(f"bank{i}", [P, 512], f32)) for i in range(8)]
        bank_free = [[] for _ in range(8)]

        def f(ap):
            return ap.bitcast(f32)

        def take_bank(*banks):
            for b in banks:
                PE.wait(*bank_free[b])
                bank_free[b] = []

        def mm(o, l, r, first, final):
            PE.quiet(lambda e: e.matmul(o, l, r, start=first, stop=final))

        def mm_end(o, l, r, first, final, *tokens):
            return PE.do(lambda e: e.matmul(o, l, r, start=first, stop=final), *tokens)

        def three(o, lH, lL, rH, rL, first, final):
            mm(o, lH, rH, first, False)
            mm(o, lH, rL, False, False)
            return mm_end(o, lL, rH, False, final)

        def flip(b, col, src, *tokens, rows=P, cols=P):
            return PE.do(lambda e: e.transpose(bank[b][0:cols, col:col + rows], src, ident[0:rows, 0:rows]),
                         *tokens)

        def part(src, high, low, *tokens, col=None):
            if col is None:
                th = ACTE.do(lambda e: e.activation(high, src, ACT.Copy), *tokens)
                tl = DVE.do(lambda e: e.tensor_tensor(low, src, f(high), ALU.subtract), th)
            else:
                th = ACTE.do(lambda e: e.activation(high, src, ACT.Identity, bias=col), *tokens)
                tl = DVE.do(lambda e: e.scalar_tensor_tensor(low, src, col, f(high), ALU.add, ALU.subtract), th)
            return th, tl

        kv_dram = nc.dram_tensor("kv_scratch", (B, P, 2 * NS + 2 * NV), f32).ap()
        wq_dram = nc.dram_tensor("wq_scratch", (KD, P, 2, KD, P), f32).ap()
        wo_dram = nc.dram_tensor("wo_scratch", (P, 2 * KD * D), f32).ap()
        w2_dram = nc.dram_tensor("w2_scratch", (P, 2 * KD * D), f32).ap()
        mlp_dram = nc.dram_tensor("mlp_scratch", (FB, P, SLOT), f32).ap()
        exp_dram = nc.dram_tensor("expert_scratch", (EB, P, 4 * D), f32).ap()
        x1_dram = nc.dram_tensor("x1_scratch", (2, P, TT, D), f32).ap()

        ident = sb("ident", [P, P])
        bias_col = sb("bias_col", [P, 2 * KD + 2 * FB])
        bo_row, bd_row = sb("bo_row", [P, D]), sb("bd_row", [P, D])
        iota = sb("iota", [P, NK, TOP], bf16)
        bound = sb("bound", [P, 1])
        t_id0 = POOL.do(lambda e: e.memset(ident[:, :], 0.0))
        t_id = POOL.do(lambda e: e.affine_select(out=ident[:, :], in_=ident[:, :], compare_op=ALU.not_equal,
                                                 fill=1.0, base=0, pattern=[[-1, P]], channel_multiplier=1), t_id0)
        POOL.do(lambda e: e.iota(iota[:, :, :], pattern=[[1, NK], [0, TOP]], base=0, channel_multiplier=0,
                                 allow_small_or_imprecise_dtypes=True))
        POOL.do(lambda e: e.memset(bound[:, :], (TOP - 0.5) * math.log(2.0)))

        xt = sb("xt", [P, TT, D])
        early = ExitStack()

        def tmp(name, shape, dt=f32):
            return early.enter_context(nc.sbuf_tensor(name, shape, dt))

        d_const, d_kv = dma("s_const"), dma("s_kv")
        d_image = {n: dma(f"s_image_{n}") for n in ("q", "o", "2")}
        d_pieces, d_ctx, d_keys = dma("s_pieces"), dma("s_ctx"), dma("s_keys")
        mats = {"k": aWk, "v": aWv, "q": aWq, "o": aWo, "2": rWq}
        wraw = {n: tmp(f"raw_{n}", [P, KD, D]) for n in mats}
        d_mat = {n: dma(f"s_raw_{n}") for n in mats}
        braw = tmp("braw", [P, P])
        bv_row = tmp("bv_row", [P, D])
        craw = tmp("craw", [P, B, D])
        t_c = d_ctx.start(SP, craw[0:S, :, :], ctx_in.rearrange("b s d -> s b d"))
        d_x = dma("s_x")
        x_v = x.rearrange("b (s t p) d -> (b s) p t d", t=TT, p=P)
        t_mat = {"k": d_mat["k"].start(SP, wraw["k"][:, :, :], aWk.rearrange("(k p) n -> p k n", p=P))}
        nb = 2 * KD + 2 * FB
        at = 0
        for src, n in ((abq, KD), (abk, KD), (bg, FB), (bu, FB)):
            d_const.start(SP, braw[at:at + n, :], src.rearrange("(n p) -> n p", p=P))
            at += n
        for dst, src in ((bo_row, abo), (bd_row, bd), (bv_row, abv)):
            t_b = d_const.start(SP, dst[:, :], src.unsqueeze(0).to_broadcast([P, D]))
        for n in ("v", "q", "o", "2"):
            t_mat[n] = d_mat[n].start(SP, wraw[n][:, :, :], mats[n].rearrange("(k p) n -> p k n", p=P))
        x_sent = {0: d_x.start(SP, xt[:, :, :], x_v[0])}
        kblk = tmp("kblk", [P, KD * P])
        keyT = tmp("keyT", [P, KD * P])
        rqT = tmp("rqT", [P, 2, KD * P])
        wkvT = tmp("wkvT", [P, 2, KD, D])
        cT = tmp("cT", [P, B, KD * S])
        vrow = tmp("vrow", [P, B, D])
        kbd = tmp("kbd", [P, NS])
        vexp = tmp("vexp", [P, NV])
        kbdH, kbdL = tmp("kbdH", [P, NS], f32r), tmp("kbdL", [P, NS], f32r)
        vexH, vexL = tmp("vexH", [P, NV], f32r), tmp("vexL", [P, NV], f32r)
        image = {n: (tmp(f"img{n}H", [P, KD, D], f32r), tmp(f"img{n}L", [P, KD, D], f32r)) for n in ("q", "o", "2")}

        t_kz = DVE.do(lambda e: e.memset(kblk[:, :], 0.0))
        t_f = flip(7, 0, braw[0:nb, :], t_b, t_id, rows=nb, cols=P)
        t_bias = DVE.do(lambda e: e.tensor_copy(bias_col[:, :], bank[7][:, 0:nb]), t_f)
        bank_free[7] = [t_bias]
        bq_c = [bias_col[:, k:k + 1] for k in range(KD)]
        bk_c = [bias_col[:, KD + k:KD + k + 1] for k in range(KD)]
        bg_c = [bias_col[:, 2 * KD + k:2 * KD + k + 1] for k in range(FB)]
        bu_c = [bias_col[:, 2 * KD + FB + k:2 * KD + FB + k + 1] for k in range(FB)]
        for q in range(KD):
            for r in range(2):
                p_, h = (2 * q + r) // H, (2 * q + r) % H
                t_kp = d_keys.start(SP, kblk[r * NK:(r + 1) * NK, q * P + r * NK:q * P + (r + 1) * NK],
                                    rkeys[h, :, p_, :], t_kz)

        for w, n in enumerate(("k", "v")):
            for k in range(KD):
                take_bank(k)
                for r in range(KD):
                    t_f = flip(k, r * P, wraw[n][:, r, k * P:(k + 1) * P], t_mat[n])
                if k % 2:
                    t_w = ACTE.do(lambda e: e.activation(wkvT[:, w, k, :], bank[k][:, :], ACT.Copy), t_f)
                else:
                    t_w = t_w0 = DVE.do(lambda e: e.tensor_copy(wkvT[:, w, k, :], bank[k][:, :]), t_f)
                bank_free[k] = [t_w]
            t_wT = [t_w, t_w0]
        for b_ in range(B):
            take_bank(4)
            for k in range(KD):
                t_f = flip(4, k * S, craw[0:S, b_, k * P:(k + 1) * P], t_c, rows=S, cols=P)
            t_cT = DVE.do(lambda e: e.tensor_copy(cT[:, b_, :], bank[4][:, 0:KD * S]), t_f)
            bank_free[4] = [t_cT]
            c3 = cT[:, b_, :].rearrange("p (k n) -> p k n", k=KD)
            take_bank(5)
            PE.wait(*t_wT)
            for k in range(KD):
                t_v = mm_end(bank[5][0:S, :], c3[:, k, :], wkvT[:, 1, k, :], k == 0, k == KD - 1, t_cT)
            t_v = DVE.do(lambda e: e.tensor_tensor(vrow[0:S, b_, :], bank[5][0:S, :], bv_row[0:S, :], ALU.add), t_v, t_b)
            bank_free[5] = [t_v]
            t_z = DVE.do(lambda e: e.memset(vexp[:, :], 0.0), ACTE.last())
            for h in range(NH):
                r = h * S
                while r < (h + 1) * S:
                    c = r // P
                    n = min((h + 1) * S, (c + 1) * P) - r
                    col = PAIRS.index((c, h // HG)) * P + (h % HG) * E
                    t_p = d_pieces.start(SP, vexp[r - c * P:r - c * P + n, col:col + E],
                                         vrow[r - h * S:r - h * S + n, b_, h * E:(h + 1) * E], t_v, t_z)
                    r += n
            t_k0 = DVE.do(lambda e: e.memset(kbd[:, :], 0.0), ACTE.last())
            for g in range(KD):
                b = 6 + g % 2
                take_bank(b)
                for k in range(KD):
                    t_k = mm_end(bank[b][:, 0:S], wkvT[:, 0, k, g * P:(g + 1) * P], c3[:, k, :], k == 0, k == KD - 1)
                for r in range(HG):
                    rows = slice(r * E, (r + 1) * E)
                    col = g * SW + r * S
                    t_kb = DVE.do(lambda e: e.tensor_scalar(
                        kbd[rows, col:col + S], bank[b][rows, 0:S], bk_c[g][rows, :], None, ALU.add), t_k, t_k0)
                bank_free[b] = [t_kb]
            t_saved = (d_kv.sem, d_kv.count) if b_ else None
            DVE.wait(t_saved)
            th, tl = part(kbd[:, :], kbdH[:, :], kbdL[:, :], t_kb, t_saved)
            o = 0
            for src in (kbdH, kbdL):
                d_kv.start(SP, kv_dram[b_, :, o:o + NS], f(src[:, :]), th, tl)
                o += NS
            th, tl = part(vexp[:, :], vexH[:, :], vexL[:, :], t_p)
            for src in (vexH, vexL):
                t_kv_saved = d_kv.start(SP, kv_dram[b_, :, o:o + NV], f(src[:, :]), th, tl)
                o += NV

        take_bank(4)
        for q in range(KD):
            t_f = flip(4, q * P, kblk[:, q * P:(q + 1) * P], t_kp)
        t_keyT = DVE.do(lambda e: e.tensor_copy(keyT[:, :], bank[4][:, :]), t_f)
        bank_free[4] = [t_keyT]
        t_images = []
        for n in ("q", "o", "2"):
            imgH, imgL = image[n]
            for k in range(KD):
                b = k
                take_bank(b)
                if n != "2":
                    for r in range(KD):
                        t_f = flip(b, r * P, wraw[n][:, r, k * P:(k + 1) * P], t_mat[n])
                else:
                    bb = 4 + k % 2
                    take_bank(bb)
                    for q in range(KD):
                        t_f = flip(bb, q * P, wraw[n][:, k, q * P:(q + 1) * P], t_mat[n])
                    t_r = DVE.do(lambda e: e.tensor_copy(rqT[:, k % 2, :], bank[bb][:, :]), t_f)
                    bank_free[bb] = [t_r]
                    for q in range(KD):
                        c = slice(q * P, (q + 1) * P)
                        t_f = mm_end(bank[b][:, c], rqT[:, k % 2, c], keyT[:, c], True, True, t_r, t_keyT)
                th, tl = part(bank[b][:, :], imgH[:, k, :], imgL[:, k, :], t_f)
                bank_free[b] = [th, tl]
            for i, src in enumerate((imgH, imgL)):
                if n == "q":
                    for g in range(KD):
                        t_image = d_image[n].start(SP, wq_dram[g, :, i, :, :], f(src[:, :, g * P:(g + 1) * P]), th, tl)
                else:
                    dst = wo_dram if n == "o" else w2_dram
                    t_image = d_image[n].start(SP, dst[:, i * KD * D:(i + 1) * KD * D],
                                            f(src[:, :, :]).rearrange("p k n -> p (k n)"), th, tl)
            t_images.append(t_image)
        everyone = [PE.last(), DVE.last(), ACTE.last(), POOL.last(), *t_images, t_kv_saved]
        for e in (PE, DVE, ACTE, POOL):
            e.wait(*everyone[:4], *t_images[:2], t_kv_saved)
        SP.wait(*everyone)
        early.close()

        ROOM = [2 * KD * ST, 2 * KD * ST, 4 * ST]
        with ExitStack() as plain:
            z_plain0, z_plain1, narrow_plain = (
                plain.enter_context(nc.sbuf_tensor(f"plain{i}", [P, n], f32)) for i, n in enumerate(ROOM))
        z_plain = [z_plain0, z_plain1]
        z_room = [sb(f"zT{i}", [P, ROOM[i]], f32r) for i in range(2)]
        narrow = sb("narrow", [P, ROOM[2]], f32r)
        ring = [sb(f"ring{i}", [P, SLOT], f32r) for i in range(RING)]
        raw = result = [sb(f"raw{i}", [P, D]) for i in range(TT)]
        keysH, keysL = sb("keysH", [P, NS], f32r), sb("keysL", [P, NS], f32r)
        valsH, valsL = sb("valsH", [P, NV], f32r), sb("valsL", [P, NV], f32r)
        zTs = [tuple(z[:, o:o + KD * ST].rearrange("p (k t) -> p k t", k=KD) for o in (0, KD * ST)) for z in z_room]
        wide = sb("wide", [P, 2 * KD * ST], f32r)
        qH = wide[:, 0:KD * ST].rearrange("p (k t) -> p k t", k=KD)
        qL = wide[:, KD * ST:2 * KD * ST].rearrange("p (k t) -> p k t", k=KD)
        turned = [(narrow[:, 2 * c * ST:(2 * c + 1) * ST], narrow[:, (2 * c + 1) * ST:(2 * c + 2) * ST]) for c in range(2)]
        sims = [narrow_plain[:, t * D:(t + 1) * D] for t in range(TT)]
        last_probs = sb("last_probs", [P, NS])
        zn = sb("zn", [P, D])
        gate = [sb(f"gate{i}", [P, ST]) for i in range(2)]
        hidH = [sb(f"hid{i}H", [P, ST], f32r) for i in range(2)]
        hidL = [sb(f"hid{i}L", [P, ST], f32r) for i in range(2)]
        dense = [sb(f"dense{i}", [P, TT * P]) for i in range(2)]
        kept = [sb(f"kept{i}", [P, TT * P], bf16) for i in range(1 + 2 * (H // 2))]
        spreadV, spreadG = sb("spreadV", [P, TT * P]), sb("spreadG", [P, TT * P])
        firsts = [sb(f"firsts{i}", [P, TT, H * NX]) for i in range(2)]
        seconds = [sb(f"seconds{i}", [P, TT, H * NK]) for i in range(2)]
        bounds = [sb(f"bounds{i}", [P, TT, H * NX], bf16) for i in range(2)]
        codes = [sb(f"codes{i}", [P, TT, H * NK * IB], bf16) for i in range(2)]
        clamps = sb("clamps", [P, 2, TT])
        stats = sb("stats", [P, 2, 6])
        mv = sb("mv", [P, TT, 2])
        std, rstd = sb("std", [P, TT]), sb("rstd", [P, TT])
        mx, den, rden = (sb(n, [P, NH]) for n in ("mx", "den", "rden"))
        HT, HC = H * TOP, H * TOP * TOP
        assert 2 * H * TOP * NX == H * TOP * NK
        top = sb("top", [P, 2 * HT])
        index = sb("index", [P, 2 * HT], mybir.dt.uint32)
        index_f = sb("index_f", [P, 2 * HT], bf16)
        cand = sb("cand", [P, HC])
        left = sb("left", [P, HC])
        weight = sb("weight", [P, HC])
        best, row, beyond, counted = (sb(n, [P, HT]) for n in ("best", "row", "beyond", "counted"))
        count = sb("count", [P, HT], bf16)
        total, inv = sb("total", [P, H]), sb("inv", [P, H])
        onehot = sb("onehot", [P, H * TOP * NX], bf16)

        NB = FB + EB
        MLP, EXPERT = 0, 1
        counters, mixed = {MLP: 0, EXPERT: 0}, []
        for letter in MIX:
            kind = MLP if letter == "M" else EXPERT
            mixed.append((kind, counters[kind]))
            counters[kind] += 1
        assert counters == {MLP: FB, EXPERT: EB}
        lead = [(MLP, j) for j in range(LEAD)]
        for j in range(EB):
            lead += [(EXPERT, j)] + ([(MLP, j + LEAD)] if j + LEAD < FB else [])
        order = lead + mixed * (NST - 1)
        d_ring = [dma(f"s_ring{i}") for i in range(RING)]
        d_second = [dma(f"s_second{i}") for i in range(RING)]
        d_save = [dma(f"s_save{i}") for i in range(RING)]
        d_raw = [dma(f"s_raw{i}") for i in range(TT)]
        slot_ready, second_ready, slot_free, t_written, made = {}, {}, [None] * RING, {}, {}
        raw_free, raw_sent, raw_used = [[] for _ in range(TT)], [], [0]
        raw_order = []
        for kind, m in lead:
            cols = slice(m * P, (m + 1) * P)
            if kind == MLP:
                for W in (Wg, Wu):
                    raw_order.append([(lambda r: r[:, :].rearrange("p (k n) -> p k n", k=KD),
                                       W[:, cols].rearrange("(k p) n -> p k n", p=P))])
                raw_order.append([(lambda r: r[:, :], Wd[cols, :])])
            else:
                for W in (down, up):
                    raw_order.append([(lambda r, a=a: r[a:P:IB, :], W[m * P + a * NK:m * P + (a + 1) * NK, :])
                                      for a in range(IB)])

        def send_raw():
            n = len(raw_sent)
            if n < len(raw_order):
                for dst, src in raw_order[n]:
                    t_sent = d_raw[n % TT].start(SP, dst(raw[n % TT]), src, *raw_free[n % TT])
                raw_sent.append(t_sent)

        def make_slot(n):
            s = n % RING
            mlp, j = order[n][0] == MLP, order[n][1]
            firsts_ = 2 if mlp else 1
            tokens = []
            for c in range(firsts_ + 1):
                r = raw_used[0]
                raw_used[0] += 1
                high, low = (c * D, (firsts_ + c) * D) if c < firsts_ else (SECOND, SECOND + D)
                hi, lo = ring[s][:, high:high + D], ring[s][:, low:low + D]
                free = [slot_free[s], made.get(n - RING)]
                DVE.wait(*free)
                if not mlp and c == 0:
                    b = 5
                    take_bank(b)
                    for k in range(KD):
                        t_f = flip(b, k * P, raw[r % TT][:, k * P:(k + 1) * P], raw_sent[r])
                    th, tl = part(bank[b][:, :], hi, lo, t_f, *free)
                    bank_free[b] = [th, tl]
                    raw_free[r % TT] = [t_f]
                else:
                    src = raw[r % TT][:, :]
                    th = ACTE.do(lambda e: e.activation(hi, src, ACT.Copy), raw_sent[r], *free)
                    tl = POOL.do(lambda e: e.tensor_tensor(lo, src, f(hi), ALU.subtract), th, *free)
                    raw_free[r % TT] = [th, tl]
                tokens += [th, tl]
                send_raw()
                if c < firsts_:
                    yield
            slot_ready[n] = second_ready[n] = tokens
            dst = mlp_dram[j] if mlp else exp_dram[j]
            o = 2 * firsts_ * D
            d_save[s].start(SP, dst[:, 0:o], f(ring[s][:, 0:o]), *tokens)
            t_written[order[n]] = made[n] = d_save[s].start(SP, dst[:, o:o + 2 * D], f(ring[s][:, SECOND:SLOT]), *tokens)

        making = []

        def make_piece():
            if making and next(making[0], "done") == "done":
                making.pop(0)

        def fill_first(n, t_free):
            if NB <= n < NB * NST:
                s, (kind, j) = n % RING, order[n]
                src, o = (mlp_dram[j], 4 * D) if kind == MLP else (exp_dram[j], 2 * D)
                slot_ready[n] = [d_ring[s].start(SP, f(ring[s][:, 0:o]), src[:, 0:o],
                                                 t_free, t_written[order[n]], made.get(n - RING))]

        def fill_second(n):
            if n < NB:
                making.append(make_slot(n))
            elif n < NB * NST:
                s, (kind, j) = n % RING, order[n]
                src, o = (mlp_dram[j], 4 * D) if kind == MLP else (exp_dram[j], 2 * D)
                second_ready[n] = [d_second[s].start(SP, f(ring[s][:, SECOND:SLOT]), src[:, o:o + 2 * D],
                                                     slot_free[s], t_written[order[n]], made.get(n - RING))]

        out_v = out.rearrange("b (s t p) d -> (b s) p t d", t=TT, p=P)
        d_x1 = dma("s_x1")
        d_wq = [dma(f"s_wq{i}") for i in range(2)]
        d_wide = dma("s_wide")
        d_res = [dma(f"s_res{i}") for i in range(TT)]
        d_out = [dma(f"s_out{i}") for i in range(TT)]
        x1_saved, retrieved, spread_done = {}, {}, {}

        stats_used, zn_used = [[], []], [None, None]

        def statistics(t, *tokens):
            ts = DVE.do(lambda e: e.bn_stats(stats[:, t % 2, :], xt[:, t, :]), *tokens, *stats_used[t % 2])
            tm = DVE.do(lambda e: e.bn_aggr(mv[:, t, :], stats[:, t % 2, :]), ts, zn_used[0])
            stats_used[t % 2] = [tm]
            return tm

        def normalise(zT, tm, t_z, row, t_row):
            te = DVE.do(lambda e: e.tensor_scalar(std[:, :], mv[:, :, 1], EPS, None, ALU.add), tm, zn_used[0])
            tq = ACTE.do(lambda e: e.activation(std[:, :], std[:, :], ACT.Sqrt), te)
            yield
            t_std = DVE.do(lambda e: e.reciprocal(rstd[:, :], std[:, :]), tq)

            def centre(t):
                tz = zn_used[0] = DVE.do(lambda e: e.tensor_scalar(
                    zn[:, :], xt[:, t, :], mv[:, t, 0:1], rstd[:, t:t + 1], ALU.subtract, ALU.mult), t_std, zn_used[1])
                t_row.append(POOL.do(lambda e: e.tensor_tensor(xt[:, t, :], xt[:, t, :], row[:, :], ALU.add), tz))
                return tz

            tz = centre(0)
            yield
            for t in range(TT):
                b = 6 + t % 2
                take_bank(b)
                for k in range(KD):
                    zn_used[1] = flip(b, k * P, zn[:, k * P:(k + 1) * P], tz)
                t_f = zn_used[1]
                if t + 1 < TT:
                    tz = centre(t + 1)
                tok = slice(t * P, (t + 1) * P)
                src = bank[b][:, :].rearrange("p (k t) -> p k t", k=KD)
                th, tl = part(src, zT[0][:, :, tok], zT[1][:, :, tok], t_f)
                bank_free[b] = [th, tl]
                t_z.append([th, tl])
                yield

        def save_x1(i):
            x1_saved[i] = d_x1.start(SP, x1_dram[i % 2], xt[:, :, :], *attended[i][2])

        def send_x(i):
            x_sent[i] = d_x.start(SP, xt[:, :, :], x_v[i], x1_saved.get(i - 1), zn_used[0])

        def attention(i):
            zT = zTs[i % 2]
            t_x = x_sent.pop(i)
            if i % (NST // B) == 0:
                o = 0
                for dst, n in ((keysH, NS), (keysL, NS), (valsH, NV), (valsL, NV)):
                    d_kv.start(SP, f(dst[:, :]), kv_dram[i // (NST // B), :, o:o + n], PE.last())
                    o += n
            t_kv = (d_kv.sem, d_kv.count)

            def send_wq(g):
                c = (g % 2) * 2 * KD * P
                return d_wq[g % 2].start(SP, f(narrow[:, c:c + 2 * KD * P]),
                                         wq_dram[g].rearrange("p a k n -> p (a k n)"), PE.last(), sims_taken[0])

            t_wq = {g: send_wq(g) for g in range(2)}
            yield
            for t in range(TT):
                tm = statistics(t, t_x)
                if t % 2:
                    yield
            t_bo, t_z = [], []
            for _ in normalise(zT, tm, t_z, bo_row, t_bo):
                yield
            t_z = t_z[-1]
            for g in range(KD):
                b = 6 + g % 2
                take_bank(b)
                PE.wait(*t_z, t_wq[g])
                c = (g % 2) * 2 * KD * P
                for k in range(KD):
                    w = narrow[:, c + k * P:c + (k + 1) * P]
                    w_ = narrow[:, c + (KD + k) * P:c + (KD + k + 1) * P]
                    t_q = three(bank[b][:, :], w, w_, zT[0][:, k, :], zT[1][:, k, :], k == 0, k == KD - 1)
                th, tl = part(bank[b][:, :], qH[:, g, :], qL[:, g, :], t_q, col=bq_c[g])
                bank_free[b] = [th, tl]
                t_qs = [th, tl]
                if g + 2 < KD:
                    t_wq[g + 2] = send_wq(g + 2)
                yield

            probs = [z_plain[i % 2][:, t * NS:(t + 1) * NS] for t in range(TT - 1)] + [last_probs[:, :]]

            def scores(t, half):
                tok = slice(t * P, (t + 1) * P)
                for g in (2 * half, 2 * half + 1):
                    b = 6 + g % 2
                    take_bank(b)
                    PE.wait(*t_qs, t_kv)
                    c = slice(g * SW, (g + 1) * SW)
                    t_s = three(bank[b][:, 0:SW], qH[:, g, tok], qL[:, g, tok], keysH[:, c], keysL[:, c], True, True)
                    v = bank[b][:, 0:SW].rearrange("p (h s) -> p h s", h=HG)
                    hs = slice(g * HG, (g + 1) * HG)
                    t_m = DVE.do(lambda e: e.tensor_reduce(mx[:, hs], v, AX.X, ALU.max), t_s, mx_used[0])
                    mx_used[0] = t_d = DVE.do(lambda e: e.tensor_tensor(
                        probs[t][:, c].rearrange("p (h s) -> p h s", h=HG), v,
                        mx[:, hs].unsqueeze(2).to_broadcast([P, HG, S]), ALU.subtract), t_m)
                    bank_free[b] = [t_d]
                return t_d

            def weigh(t, t_d):
                p3 = probs[t].rearrange("p (h s) -> p h s", h=NH)
                yield
                t_e = ACTE.do(lambda e: e.activation(probs[t], probs[t], ACT.Exp, scale=E ** -0.5), t_d)
                yield
                t_n = DVE.do(lambda e: e.tensor_reduce(den[:, :], p3, AX.X, ALU.add), t_e, den_used[0])
                t_r = den_used[0] = DVE.do(lambda e: e.reciprocal(rden[:, :], den[:, :]), t_n, rden_used[0])
                rden_used[0] = (DVE if t == TT - 1 else POOL).do(lambda e: e.tensor_tensor(
                    p3, p3, rden[:, :].unsqueeze(2).to_broadcast([P, NH, S]), ALU.mult), t_r)
                t_probs.append(rden_used[0])

            t_probs, weighing = [], iter(())
            for t in range(TT):
                scores(t, 0)
                next(weighing, None)
                yield
                t_d = scores(t, 1)
                next(weighing, None)
                weighing = weigh(t, t_d)
                next(weighing)
                yield
            for _ in weighing:
                yield
            yield

            def turn(c):
                n = min(P, NS - c * P)
                take_bank(7)
                for t in range(TT):
                    t_f = flip(7, t * P, probs[t][:, c * P:c * P + n], t_probs[t], cols=n)
                hi, lo = turned[c % 2]
                th, tl = part(bank[7][0:n, :], hi[0:n, :], lo[0:n, :], t_f)
                bank_free[7] = [th, tl]
                return [th, tl]

            yield
            t_turned = {0: turn(0)}
            t_att = {}
            for m, (c, g) in enumerate(PAIRS):
                yield
                if c + 1 < NC and c + 1 not in t_turned:
                    t_turned[c + 1] = turn(c + 1)
                first, final = m == 0 or PAIRS[m - 1][1] != g, m + 1 == len(PAIRS) or PAIRS[m + 1][1] != g
                if first:
                    take_bank(6)
                PE.wait(*t_turned[c])
                n = min(P, NS - c * P)
                v = slice(m * P, (m + 1) * P)
                hi, lo = turned[c % 2]
                t_o = three(bank[6][:, :], valsH[0:n, v], valsL[0:n, v], hi[0:n, :], lo[0:n, :], first, final)
                if final:
                    t_att[g] = part(bank[6][:, :], qH[:, g, :], qL[:, g, :], t_o)
                    bank_free[6] = [*t_att[g]]
            wo = z_room[i % 2]
            t_w = d_wide.start(SP, f(wo[:, :]), wo_dram, PE.last())
            yield
            yield
            yield
            yield
            for t in range(TT):
                tok = slice(t * P, (t + 1) * P)
                b = 6 + t % 2
                take_bank(b)
                PE.wait(*t_att[KD - 1], t_w)
                for k in range(KD):
                    t_y = three(bank[b][:, :], qH[:, k, tok], qL[:, k, tok], wo[:, k * D:(k + 1) * D],
                                wo[:, (KD + k) * D:(KD + k + 1) * D], k == 0, k == KD - 1)
                t_x1 = DVE.do(lambda e: e.tensor_tensor(xt[:, t, :], bank[b][:, :], xt[:, t, :], ALU.add), t_y, t_bo[t])
                bank_free[b] = [t_x1]
                tm = statistics(t, t_x1)
                yield
            t_w = d_wide.start(SP, f(wide[:, :]), w2_dram, PE.last())
            t_z2, t_bd = [], []
            for _ in normalise(zT, tm, t_z2, bd_row, t_bd):
                yield
            t_sim = []
            for t in range(TT):
                tok = slice(t * P, (t + 1) * P)
                b = 6 + t % 2
                take_bank(b)
                PE.wait(*t_z2[t], t_w)
                for k in range(KD):
                    t_y = three(bank[b][:, :], zT[0][:, k, tok], zT[1][:, k, tok], wide[:, k * D:(k + 1) * D],
                                wide[:, (KD + k) * D:(KD + k + 1) * D], k == 0, k == KD - 1)
                t_c = ACTE.do(lambda e: e.activation(sims[t], bank[b][:, :], ACT.Copy), t_y)
                bank_free[b] = [t_c]
                t_sim.append(t_c)
                yield
            attended[i] = (t_sim, t_z2, t_bd)

        mx_used, den_used, rden_used = [None], [None], [None]
        attended, sims_taken = {}, [None]

        def retrieval(i, t):
            V = DVE.do
            i_ = i % 2
            first, second = firsts[i_][:, t, :], seconds[i_][:, t, :]
            code = codes[i_][:, t, :].rearrange("p (h j i) -> p h j i", h=H, i=IB)
            bound_i = bounds[i_][:, t, :]
            t_sim = attended[i][0][t]
            sim = sims[t].rearrange("p (g n) -> p g n", g=2 * H)
            top3 = top[:, :].rearrange("p (g n) -> p g n", g=2 * H)
            for half in range(2):
                gs = range(half * H, (half + 1) * H)
                for g in gs:
                    t1 = V(lambda e: e.max(top3[:, g, :], sim[:, g, :]), t_sim)
                for g in gs:
                    t1 = V(lambda e: e.max_index(index[:, g * TOP:(g + 1) * TOP], top3[:, g, :], sim[:, g, :]), t1)
                yield
            t1 = V(lambda e: e.tensor_copy(index_f[:, :], index[:, :]), t1)
            t5 = V(lambda e: e.tensor_tensor(
                first.rearrange("p (h n) -> p h n", h=H), sim[:, 0:H, 0:NX],
                top3[:, 0:H, 0:1].to_broadcast([P, H, NX]), ALU.subtract), t1, *spread_done.get(i - 2, []))
            t5 = V(lambda e: e.tensor_tensor(
                second.rearrange("p (h n) -> p h n", h=H), sim[:, H:2 * H, :],
                top3[:, H:2 * H, 0:1].to_broadcast([P, H, NK]), ALU.subtract), t5)
            c4 = cand[:, :].rearrange("p (h a b) -> p h a b", h=H, a=TOP)
            for h in range(H):
                t2 = V(lambda e: e.tensor_tensor(
                    c4[:, h, :, :], top3[:, h, :].unsqueeze(2).to_broadcast([P, TOP, TOP]),
                    top3[:, H + h, :].unsqueeze(1).to_broadcast([P, TOP, TOP]), ALU.add), t1)
            c2 = cand[:, :].rearrange("p (h n) -> p h n", h=H)
            l2 = left[:, :].rearrange("p (h n) -> p h n", h=H)
            b2 = best[:, :].rearrange("p (h n) -> p h n", h=H)
            for h in range(H):
                t3 = V(lambda e: e.max(b2[:, h, :], c2[:, h, :]), t2)
            yield
            for h in range(H):
                t3 = V(lambda e: e.match_replace(l2[:, h, :], b2[:, h, :], c2[:, h, :], FAR), t3)
            t4 = V(lambda e: e.tensor_tensor(weight[:, :].rearrange("p (h n) -> p h n", h=H), c2,
                                             b2[:, :, 0:1].to_broadcast([P, H, TOP * TOP]), ALU.subtract), t3)
            yield
            t4 = ACTE.do(lambda e: e.activation(weight[:, :], weight[:, :], ACT.Exp), t4)
            ta = ACTE.do(lambda e: e.activation(first, first, ACT.Exp), t5)
            tb = ACTE.do(lambda e: e.activation(second, second, ACT.Exp), t5)
            t3 = V(lambda e: e.tensor_tensor(left[:, :], left[:, :], cand[:, :], ALU.is_lt), t3)
            t_n = V(lambda e: e.tensor_reduce(counted[:, :], left[:, :].rearrange("p (r n) -> p r n", n=TOP), AX.X, ALU.add), t3)
            t_n = V(lambda e: e.tensor_copy(count[:, :], counted[:, :]), t_n)
            one = onehot[:, :].rearrange("p (h i r) -> p h i r", h=H, r=TOP)
            t9 = V(lambda e: e.tensor_tensor(
                one, iota[:, 0:NX, :].unsqueeze(1).to_broadcast([P, H, NX, TOP]),
                index_f[:, 0:HT].rearrange("p (h r) -> p h r", h=H).unsqueeze(2).to_broadcast([P, H, NX, TOP]),
                ALU.is_equal), t1)
            t9 = V(lambda e: e.tensor_tensor(
                one, one, count[:, :].rearrange("p (h r) -> p h r", h=H).unsqueeze(2).to_broadcast([P, H, NX, TOP]),
                ALU.mult), t9, t_n)
            yield
            for n in (4, 2):
                t9 = V(lambda e: e.tensor_tensor(one[:, :, :, 0:n], one[:, :, :, 0:n], one[:, :, :, n:2 * n], ALU.add), t9)
            t9 = V(lambda e: e.tensor_tensor(bound_i.rearrange("p (h i) -> p h i", h=H),
                                             one[:, :, :, 0], one[:, :, :, 1], ALU.add), t9)
            yield
            t_b = ACTE.do(lambda e: e.activation(bound_i, bound_i, ACT.Exp, bias=bound[:, :], scale=-math.log(2.0)), t9)
            t4 = V(lambda e: e.tensor_tensor(weight[:, :], weight[:, :], left[:, :], ALU.mult), t4, t3)
            t4 = V(lambda e: e.tensor_reduce(row[:, :], weight[:, :].rearrange("p (r n) -> p r n", n=TOP), AX.X, ALU.add), t4)
            t6 = V(lambda e: e.tensor_reduce(total[:, :], row[:, :].rearrange("p (h n) -> p h n", h=H), AX.X, ALU.add), t4)
            t6 = V(lambda e: e.reciprocal(inv[:, :], total[:, :]), t6)
            t8 = V(lambda e: e.tensor_tensor(first.rearrange("p (h n) -> p h n", h=H), first.rearrange("p (h n) -> p h n", h=H),
                                             inv[:, :].unsqueeze(2).to_broadcast([P, H, NX]), ALU.mult), ta, t6)
            t7 = V(lambda e: e.scalar_tensor_tensor(beyond[:, :], index_f[:, 0:HT], float(NX), row[:, :],
                                                    ALU.is_ge, ALU.mult), t6)
            b3 = beyond[:, :].rearrange("p (h n) -> p h n", h=H)
            t7 = V(lambda e: e.tensor_tensor(b3, b3, inv[:, :].unsqueeze(2).to_broadcast([P, H, TOP]), ALU.mult), t7)
            t7 = V(lambda e: e.tensor_reduce(clamps[:, i_, t:t + 1], beyond[:, :], AX.X, ALU.add), t7)
            yield
            one = onehot[:, :].rearrange("p (h j r) -> p h j r", h=H // 2, r=TOP)
            tc = t9
            for pair in range(2):
                hs = slice(pair * (H // 2), (pair + 1) * (H // 2))
                tc = V(lambda e: e.tensor_tensor(
                    one, iota[:, :, :].unsqueeze(1).to_broadcast([P, H // 2, NK, TOP]),
                    index_f[:, HT:2 * HT].rearrange("p (h r) -> p h r", h=H)[:, hs, :].unsqueeze(2).to_broadcast(
                        [P, H // 2, NK, TOP]), ALU.is_equal), tc)
                yield
                for n in (4, 2):
                    tc = V(lambda e: e.scalar_tensor_tensor(one[:, :, :, 0:n], one[:, :, :, 0:n], 2.0 ** n,
                                                            one[:, :, :, n:2 * n], ALU.mult, ALU.add), tc)
                yield
                for r in range(H // 2):
                    tc = V(lambda e: e.scalar_tensor_tensor(
                        code[:, pair * (H // 2) + r, :, :], one[:, r, :, 0:1].to_broadcast([P, NK, IB]), 2.0,
                        one[:, r, :, 1:2].to_broadcast([P, NK, IB]), ALU.mult, ALU.add), tc)
            sims_taken[0] = tc
            retrieved[i] = retrieved.get(i, []) + [tc, t8, t7, tb, t_b]
            yield

        dense_ready, dense_free = {}, [None, None]
        kept_free, v_used = [None] * len(kept), [None]

        def spread(i, eb):
            i_ = i % 2

            def shaped(a):
                return a[:, :].rearrange("p (t j i) -> p t j i", t=TT, i=IB)

            def by_first(a, h):
                o = h * NX + eb * IB
                return a[i_][:, :, o:o + IB].unsqueeze(2).to_broadcast([P, TT, NK, IB])

            def by_second(h):
                return seconds[i_][:, :, h * NK:(h + 1) * NK].unsqueeze(3).to_broadcast([P, TT, NK, IB])

            def slot(h):
                return 0 if h < H // 2 else 1 + (h - H // 2) * 2 + eb % 2

            def mask(h):
                code = codes[i_][:, :, h * NK * IB:(h + 1) * NK * IB].rearrange("p t (j i) -> p t j i", i=IB)
                return DVE.do(lambda e: e.tensor_tensor(shaped(kept[slot(h)]), code, by_first(bounds, h), ALU.is_gt),
                              *retrieved[i], kept_free[slot(h)])

            d4, v4, g4 = shaped(dense[eb % 2]), shaped(spreadV), shaped(spreadG)
            on_pool = range(H // 2, H)
            k_pool = [mask(h) for h in on_pool]
            kp = POOL.last()
            yield
            for h in range(H // 2):
                k = mask(h)
                k = DVE.do(lambda e: e.tensor_tensor(v4, shaped(kept[slot(h)]), by_first(firsts, h), ALU.mult), k, v_used[0])
                kept_free[slot(h)] = k
                yield
                if h == 0:
                    k0 = v_used[0] = DVE.do(lambda e: e.tensor_tensor(d4, v4, by_second(h), ALU.mult), k, dense_free[eb % 2])
                    if eb == EB - 1:
                        last = d4[:, :, NK - 1, IB - 1]
                        k0 = DVE.do(lambda e: e.tensor_tensor(last, last, clamps[:, i_, :], ALU.add), k0)
                    yield
                else:
                    k = DVE.do(lambda e: e.tensor_tensor(v4, v4, by_second(h), ALU.mult), k)
                    k0 = v_used[0] = DVE.do(lambda e: e.tensor_tensor(d4, d4, v4, ALU.add), k, k0)
                    yield
            for h, k in zip(on_pool, k_pool):
                kp = POOL.do(lambda e: e.tensor_tensor(g4, shaped(kept[slot(h)]), by_first(firsts, h), ALU.mult), k, kp)
                kept_free[slot(h)] = kp
                kp = POOL.do(lambda e: e.tensor_tensor(g4, g4, by_second(h), ALU.mult), kp)
                kp = POOL.do(lambda e: e.tensor_tensor(d4, d4, g4, ALU.add), kp, k0)
            dense_ready[i, eb] = kp
            if eb == EB - 1:
                spread_done[i] = [kp, DVE.last()]

        def all_weights():
            for i in range(NST):
                for eb in range(EB):
                    while experts_done[0] < i * EB + eb - 1 or len(retrieved.get(i, [])) < 5 * TT:
                        yield
                    for _ in spread(i, eb):
                        yield

        def background():
            for t in range(TT):
                for _ in retrieval(0, t):
                    yield 0.5
            for i in range(1, NST):
                for _ in attention(i):
                    yield ATT_PACE if i > 1 else 0.85
                for t in range(TT):
                    for _ in retrieval(i, t):
                        yield RET_PACE if i > 1 else 0.9
                    if t == 0:
                        save_x1(i)
                    if t == 1 and i + 1 < NST:
                        send_x(i + 1)
                while current[0] < i:
                    yield 1.0

        for n in range(RING):
            fill_second(n)
        for n, _ in enumerate(attention(0)):
            if n < TT:
                send_raw()
            elif n > 12 and n % 3 == 0:
                make_piece()
        save_x1(0)
        send_x(1)

        def project(i, n, m, ready):
            nb_ = n % NB
            if nb_ == 0:
                take_bank(*range(TT))
            PE.wait(*ready, *second_ready.pop(n))
            wH, wL = (ring[n % RING][:, o:o + D] for o in (SECOND, SECOND + D))
            for t in range(TT):
                tok = slice(t * P, (t + 1) * P)
                k = three(bank[t][:, :], hidH[m][:, tok], hidL[m][:, tok], wH, wL, nb_ == 0, nb_ == NB - 1)
            slot_free[n % RING] = k
            fill_second(n + RING)
            if nb_ == NB - 1:
                finish(i, k)

        def send_back(i):
            for t in range(TT):
                t_back[t] = d_res[t].start(SP, result[t][:, :], x1_dram[i % 2, :, t, :], x1_saved[i],
                                           (d_out[t].sem, d_out[t].count), *raw_free[t])

        def finish(i, k):
            for t in range(TT):
                r = result[t]
                t_r = DVE.do(lambda e: e.tensor_tensor(r[:, :], bank[t][:, :], r[:, :], ALU.add), k, t_back[t])
                bank_free[t] = [t_r]
                d_out[t].start(SP, out_v[i][:, t, :], r[:, :], t_r)

        t_back = [None] * TT
        experts_done, current, spent = [0], [0], [0.0]
        weights, beside = all_weights(), background()

        def aside(n):
            make_piece()
            for _ in range(2 if n < NB else 1):
                next(weights, None)
            spent[0] -= 1.0
            while spent[0] < 0.0:
                spent[0] += next(beside, 1.0)

        later = None
        for n in range(NST * NB):
            i, nb_ = n // NB, n % NB
            kind, j = order[n]
            m = n % 2
            zT = zTs[i % 2]
            w = ring[n % RING]
            if nb_ == 0:
                current[0] = i
                while i not in attended:
                    next(beside)
                PE.wait(*(tok for z in attended[i][1] for tok in z))
            if nb_ == NB - 1:
                send_back(i)
            while n not in slot_ready:
                make_piece()
            take_bank(4)
            PE.wait(*slot_ready.pop(n))
            low = (2 if kind == MLP else 1) * D
            for k in range(KD):
                c = k * P
                t_g0 = three(bank[4][:, :], w[:, c:c + P], w[:, low + c:low + c + P],
                             zT[0][:, k, :], zT[1][:, k, :], k == 0, k == KD - 1)
            if kind == MLP:
                t_s = ACTE.do(lambda e: e.activation(gate[m][:, :], bank[4][:, :], ACT.Silu, bias=bg_c[j]), t_g0)
                aside(n)
                take_bank(5)
                for k in range(KD):
                    c = D + k * P
                    t_g = three(bank[5][:, :], w[:, c:c + P], w[:, low + c:low + c + P],
                                zT[0][:, k, :], zT[1][:, k, :], k == 0, k == KD - 1)
                fill_first(n + RING, t_g)
                t_h = DVE.do(lambda e: e.scalar_tensor_tensor(gate[m][:, :], bank[5][:, :], bu_c[j], gate[m][:, :],
                                                              ALU.add, ALU.mult), t_g, t_s)
            else:
                t_s = ACTE.do(lambda e: e.activation(gate[m][:, :], bank[4][:, :], ACT.Silu), t_g0)
                fill_first(n + RING, t_g0)
                aside(n)
                while (i, j) not in dense_ready:
                    next(weights)
                take_bank(5)
                for t in range(TT):
                    t_g = flip(5, t * P, dense[j % 2][:, t * P:(t + 1) * P], dense_ready[i, j])
                dense_free[j % 2] = t_g
                experts_done[0] += 1
                t_h = DVE.do(lambda e: e.tensor_tensor(gate[m][:, :], bank[5][:, :], gate[m][:, :], ALU.mult), t_g, t_s)
            bank_free[4], bank_free[5] = [t_s], [t_h]
            t_hi = ACTE.do(lambda e: e.activation(hidH[m][:, :], gate[m][:, :], ACT.Copy), t_h)
            aside(n)
            t_lo = DVE.do(lambda e: e.tensor_tensor(hidL[m][:, :], gate[m][:, :], f(hidH[m][:, :]), ALU.subtract), t_hi)
            ready = (t_hi, t_lo)
            if later:
                project(*later)
            aside(n)
            later = (i, n, m, ready)
            aside(n)
        project(*later)
        for d in (*d_out, *d_save, d_kv, *d_image.values(), d_x1):
            SP.wait((d.sem, d.count))


_INS = ["x", "ctx_1024", "L0_xattn_Wq", "L0_xattn_bq", "L0_xattn_Wk", "L0_xattn_bk", "L0_xattn_Wv", "L0_xattn_bv",
        "L0_xattn_Wo", "L0_xattn_bo", "L0_ffn_Wg", "L0_ffn_bg", "L0_ffn_Wu", "L0_ffn_bu", "L0_ffn_Wd", "L0_ffn_bd",
        "L0_ffn_Wq", "L0_ffn_keys", "L0_ffn_down_embed", "L0_ffn_up_embed"]


def kernel(**inputs):
    import numpy as np
    import concourse.bacc as bacc
    from concourse.bass_utils import run_bass_kernel_spmd

    nc = bacc.Bacc("TRN2", target_bir_lowering=False, num_devices=1)
    arrays, args = {}, []
    for name in _INS:
        a = np.ascontiguousarray(inputs[name])
        arrays[f"in_{name}"] = a
        args.append(nc.dram_tensor(f"in_{name}", a.shape, mybir.dt.from_np(a.dtype), kind="ExternalInput").ap())
    args.append(nc.dram_tensor("out_0", (B, T, D), mybir.dt.float32, kind="ExternalOutput").ap())
    program(nc, *args)
    r = run_bass_kernel_spmd(nc, [arrays], core_ids=[0])
    return r.results[0]["out_0"]
```
